# Optimizing a Trainium2 kernel written in Bass

```python
import numpy as np
import jax
import jax.numpy as jnp

def _softmax(x, axis=-1):
    return jax.nn.softmax(x, axis=axis)

def _gelu(x):
    return jax.nn.gelu(x, approximate=True)

def _silu(x):
    return jax.nn.silu(x)

def _sigmoid(x):
    return jax.nn.sigmoid(x)

def _layernorm(x, axis=-1, eps=1e-05):
    m = jnp.mean(x, axis=axis, keepdims=True)
    v = jnp.var(x, axis=axis, keepdims=True)
    return (x - m) / jnp.sqrt(v + eps)

def _scatter_add(tgt, idx, src, axis=0):
    return tgt.at[idx].add(src)

def _segment_sum(src, seg, n):
    return jax.ops.segment_sum(src, seg, n)
kernel_name = 'mk_xattn_ffn_d1_seqx_r8_60aa10'

def setup_inputs(seed: int=0):
    np.random.seed(seed)
    _w = jnp.asarray

    def _rec_inputs():
        import jax
        import jax.numpy as jnp
        _rk = jax.random.key(seed)
        x = -0.0003929 + 0.9999 * jax.random.normal(jax.random.fold_in(_rk, 1), (32, 64, 256), jnp.float32)
        _lenS = 64 - jax.random.randint(jax.random.fold_in(_rk, 7), (32,), 0, max(1, 64 // 4) + 1, jnp.int32)
        _lenS2 = 64 - jax.random.randint(jax.random.fold_in(_rk, 8), (32,), 0, max(1, 64 // 4) + 1, jnp.int32)
        _ctx_2048P = jax.random.normal(jax.random.fold_in(_rk, 11), (32, 16, 256), jnp.float32)
        _ctx_2048c = jax.random.dirichlet(jax.random.fold_in(_rk, 511), 0.3 * jnp.ones((16,), jnp.float32), (32, 64))
        _ctx_2048t = jnp.einsum('bsk,bkd->bsd', _ctx_2048c, _ctx_2048P)
        _ctx_2048t = _ctx_2048t * jax.lax.rsqrt(jnp.mean(jnp.square(_ctx_2048t)) + 1e-12) * 0.953939
        ctx_2048 = -0.000514642 + 1.00011 * (_ctx_2048t + 0.3 * jax.random.normal(jax.random.fold_in(_rk, 611), (32, 64, 256), jnp.float32))
        _validS = jnp.arange(64)[None, :] < _lenS[:, None]
        _validS2 = jnp.arange(64)[None, :] < _lenS2[:, None]
        _causal = jnp.tril(jnp.ones((64, 64), dtype=bool))
        mask_BxS2_ik0 = jnp.where(jnp.broadcast_to(_validS2[:, :], (32, 64)), 0, 1).astype(jnp.int32)
        return (x, ctx_2048, mask_BxS2_ik0)
    x, ctx_2048, mask_BxS2_ik0 = _rec_inputs()

    def _L0_xattn_setup():
        import jax, jax.numpy as jnp
        import numpy as np
        import math
        H = 256
        NH = 16
        HD = H // NH
        EPS_LN = 1e-05
        RES_SCALE_MAX = 0.3

        def _nan_clean(x, lim=10000.0):
            return jnp.nan_to_num(x, nan=0.0, posinf=lim, neginf=-lim)
        key = jax.random.key(seed)
        ks = jax.random.split(key, 12)
        B, S, T = (4, 256, 32)
        std = 1.0 / math.sqrt(H)
        return {'hidden_states': jax.random.normal(ks[0], (B, S, H), jnp.float32), 'audio_tokens': jax.random.normal(ks[1], (B, T, H), jnp.float32), 'attention_mask': jax.random.randint(ks[2], (B, T), 0, 2, jnp.int32), 'Wq': jax.random.normal(ks[3], (H, H), jnp.float32) * std, 'bq': jnp.zeros((H,), jnp.float32), 'Wk': jax.random.normal(ks[4], (H, H), jnp.float32) * std, 'bk': jnp.zeros((H,), jnp.float32), 'Wv': jax.random.normal(ks[5], (H, H), jnp.float32) * std, 'bv': jnp.zeros((H,), jnp.float32), 'Wo': jax.random.normal(ks[6], (H, H), jnp.float32) * std, 'bo': jnp.zeros((H,), jnp.float32), 'ln_gamma': jnp.ones((H,), jnp.float32), 'ln_beta': jnp.zeros((H,), jnp.float32), 'residual_scale': jnp.float32(0.05)}
    _L0_xattn_all = _L0_xattn_setup()
    _L0_xattn_in = {k: v for k, v in _L0_xattn_all.items() if k in ('Wq', 'bq', 'Wk', 'bk', 'Wv', 'bv', 'Wo', 'bo', 'ln_gamma', 'ln_beta', 'residual_scale')}
    del _L0_xattn_all

    def _L0_ffn_setup():
        import jax, jax.numpy as jnp
        import numpy as np
        NUM_EXPERTS = 8
        TOP_K = 2
        IN_DIM = 256
        BOT_DIM = 64
        BATCH, SEQ = (4, 256)

        def _gelu(x):
            return jax.nn.gelu(x, approximate=False)
        key = jax.random.key(seed)
        ks = jax.random.split(key, 8)
        scale_d = 1.0 / np.sqrt(IN_DIM)
        scale_b = 1.0 / np.sqrt(BOT_DIM)
        return {'hidden_states': jax.random.normal(ks[0], (BATCH, SEQ, IN_DIM), jnp.float32), 'gate_w': jax.random.normal(ks[1], (NUM_EXPERTS, IN_DIM), jnp.float32) * scale_d, 'wd': jax.random.normal(ks[2], (NUM_EXPERTS, BOT_DIM, IN_DIM), jnp.float32) * scale_d, 'bd': jnp.zeros((NUM_EXPERTS, BOT_DIM), jnp.float32), 'wu': jax.random.normal(ks[3], (NUM_EXPERTS, IN_DIM, BOT_DIM), jnp.float32) * scale_b * 0.02, 'bu': jnp.zeros((NUM_EXPERTS, IN_DIM), jnp.float32), 'ws_d': jax.random.normal(ks[4], (BOT_DIM, IN_DIM), jnp.float32) * scale_d, 'bs_d': jnp.zeros((BOT_DIM,), jnp.float32), 'ws_u': jax.random.normal(ks[5], (IN_DIM, BOT_DIM), jnp.float32) * scale_b * 0.02, 'bs_u': jnp.zeros((IN_DIM,), jnp.float32)}
    _L0_ffn_all = _L0_ffn_setup()
    _L0_ffn_in = {k: v for k, v in _L0_ffn_all.items() if k in ('gate_w', 'wd', 'bd', 'wu', 'bu', 'ws_d', 'bs_d', 'ws_u', 'bs_u')}
    del _L0_ffn_all
    return {'x': x, 'ctx_2048': ctx_2048, 'mask_BxS2_ik0': mask_BxS2_ik0, 'L0_xattn_Wq': _L0_xattn_in['Wq'], 'L0_xattn_bq': _L0_xattn_in['bq'], 'L0_xattn_Wk': _L0_xattn_in['Wk'], 'L0_xattn_bk': _L0_xattn_in['bk'], 'L0_xattn_Wv': _L0_xattn_in['Wv'], 'L0_xattn_bv': _L0_xattn_in['bv'], 'L0_xattn_Wo': _L0_xattn_in['Wo'], 'L0_xattn_bo': _L0_xattn_in['bo'], 'L0_xattn_ln_gamma': _L0_xattn_in['ln_gamma'], 'L0_xattn_ln_beta': _L0_xattn_in['ln_beta'], 'L0_xattn_residual_scale': _L0_xattn_in['residual_scale'], 'L0_ffn_gate_w': _L0_ffn_in['gate_w'], 'L0_ffn_wd': _L0_ffn_in['wd'], 'L0_ffn_bd': _L0_ffn_in['bd'], 'L0_ffn_wu': _L0_ffn_in['wu'], 'L0_ffn_bu': _L0_ffn_in['bu'], 'L0_ffn_ws_d': _L0_ffn_in['ws_d'], 'L0_ffn_bs_d': _L0_ffn_in['bs_d'], 'L0_ffn_ws_u': _L0_ffn_in['ws_u'], 'L0_ffn_bs_u': _L0_ffn_in['bs_u']}

def reference(x, ctx_2048, mask_BxS2_ik0, L0_xattn_Wq, L0_xattn_bq, L0_xattn_Wk, L0_xattn_bk, L0_xattn_Wv, L0_xattn_bv, L0_xattn_Wo, L0_xattn_bo, L0_xattn_ln_gamma, L0_xattn_ln_beta, L0_xattn_residual_scale, L0_ffn_gate_w, L0_ffn_wd, L0_ffn_bd, L0_ffn_wu, L0_ffn_bu, L0_ffn_ws_d, L0_ffn_bs_d, L0_ffn_ws_u, L0_ffn_bs_u):
    import jax
    import jax.numpy as jnp

    def _L0_xattn_ref(hidden_states, audio_tokens, attention_mask, Wq, bq, Wk, bk, Wv, bv, Wo, bo, ln_gamma, ln_beta, residual_scale):
        import jax, jax.numpy as jnp
        import numpy as np
        import math
        H = 256
        NH = 16
        HD = H // NH
        EPS_LN = 1e-05
        RES_SCALE_MAX = 0.3

        def _nan_clean(x, lim=10000.0):
            return jnp.nan_to_num(x, nan=0.0, posinf=lim, neginf=-lim)
        B, S, _ = hidden_states.shape
        T = audio_tokens.shape[1]
        hs = _nan_clean(hidden_states).astype(jnp.float32)
        at = _nan_clean(audio_tokens).astype(jnp.float32)

        def proj(x, W, b, L):
            y = x @ W.T + b
            return y.reshape(B, L, NH, HD).transpose(0, 2, 1, 3)
        q = _nan_clean(proj(hs, Wq, bq, S))
        k = _nan_clean(proj(at, Wk, bk, T))
        v = _nan_clean(proj(at, Wv, bv, T))
        scale = max(math.sqrt(HD), 1e-08)
        scores = jnp.einsum('bhsd,bhtd->bhst', q, k) / scale
        scores = jnp.clip(scores, -50.0, 50.0)
        scores = jnp.nan_to_num(scores, nan=0.0, posinf=50.0, neginf=-50.0)
        attend = (attention_mask.astype(jnp.float32) > 0.5)[:, None, None, :]
        scores = jnp.where(attend, scores, -10000.0)
        scores = jnp.clip(scores, -50.0, 50.0)
        probs = jax.nn.softmax(scores, axis=-1)
        probs = jnp.nan_to_num(probs, nan=0.0, posinf=1.0, neginf=0.0)
        probs = probs / (probs.sum(axis=-1, keepdims=True) + 1e-08)
        ctx = jnp.einsum('bhst,bhtd->bhsd', probs, v)
        ctx = ctx.transpose(0, 2, 1, 3).reshape(B, S, H)
        delta = _nan_clean(ctx @ Wo.T + bo)
        rs = jnp.clip(residual_scale, 0.0, RES_SCALE_MAX)
        delta = rs * delta
        mu = delta.mean(axis=-1, keepdims=True)
        var = jnp.mean((delta - mu) ** 2, axis=-1, keepdims=True)
        delta = (delta - mu) / jnp.sqrt(var + EPS_LN) * ln_gamma + ln_beta
        return delta

    def _L0_ffn_ref(hidden_states, gate_w, wd, bd, wu, bu, ws_d, bs_d, ws_u, bs_u):
        import jax, jax.numpy as jnp
        import numpy as np
        NUM_EXPERTS = 8
        TOP_K = 2
        IN_DIM = 256
        BOT_DIM = 64
        BATCH, SEQ = (4, 256)

        def _gelu(x):
            return jax.nn.gelu(x, approximate=False)
        B, S, D = hidden_states.shape
        x = hidden_states.reshape(-1, D)
        T = x.shape[0]
        logits = x @ gate_w.T
        probs = jax.nn.softmax(logits.astype(jnp.float32), axis=-1)
        rw, sel = jax.lax.top_k(probs, TOP_K)
        rw = rw / rw.sum(axis=-1, keepdims=True)
        rw = rw.astype(x.dtype)
        combine = jnp.zeros((T, NUM_EXPERTS), x.dtype).at[jnp.arange(T)[:, None], sel].add(rw)
        down = jnp.einsum('td,ebd->teb', x, wd) + bd[None]
        h = _gelu(down) * combine[:, :, None]
        expert_out = jnp.einsum('teb,edb->td', h, wu) + combine @ bu
        shared = _gelu(x @ ws_d.T + bs_d) @ ws_u.T + bs_u
        out = (expert_out + shared).reshape(B, S, D)
        return out
    x = x + _L0_xattn_ref(_layernorm(x, axis=-1), ctx_2048, mask_BxS2_ik0, L0_xattn_Wq, L0_xattn_bq, L0_xattn_Wk, L0_xattn_bk, L0_xattn_Wv, L0_xattn_bv, L0_xattn_Wo, L0_xattn_bo, L0_xattn_ln_gamma, L0_xattn_ln_beta, L0_xattn_residual_scale)
    x = x + _L0_ffn_ref(_layernorm(x, axis=-1), L0_ffn_gate_w, L0_ffn_wd, L0_ffn_bd, L0_ffn_wu, L0_ffn_bu, L0_ffn_ws_d, L0_ffn_bs_d, L0_ffn_ws_u, L0_ffn_bs_u)
    return x

_drawn_inputs = setup_inputs


def setup_inputs(seed=0):
    import zlib

    import numpy as np

    out = dict(_drawn_inputs(seed))
    spreads = {'L0_xattn_bq': (0.0, 0.1),
     'L0_xattn_bk': (0.0, 0.8),
     'L0_xattn_bv': (0.0, 0.1),
     'L0_xattn_bo': (0.0, 0.1),
     'L0_xattn_ln_gamma': (1.0, 0.2),
     'L0_xattn_ln_beta': (0.0, 0.1),
     'L0_ffn_bd': (0.0, 0.8),
     'L0_ffn_bu': (0.0, 0.1),
     'L0_ffn_bs_d': (0.0, 0.8),
     'L0_ffn_bs_u': (0.0, 0.1)}
    factors = {'L0_ffn_wd': 8.0, 'L0_ffn_wu': 8.0, 'L0_ffn_ws_d': 6.846, 'L0_ffn_ws_u': 6.072}
    for name, (base, spread) in spreads.items():
        noise = np.random.default_rng([zlib.crc32(name.encode()), seed]).standard_normal(out[name].shape)
        drawn = base * np.exp(spread * noise) if base else spread * noise
        out[name] = jnp.asarray(drawn.astype(out[name].dtype))
    for name, factor in factors.items():
        out[name] = (out[name] * factor).astype(out[name].dtype)
    return out
```

```python
import numpy as np
import concourse.bass as bass
from concourse import mybir
from contextlib import ExitStack

B, S, H = 32, 64, 256
NH, HD = 16, 16
NE, BOT = 8, 64
TOK = B * S

P = 128
KT = H // P
CH = 256
NCH = TOK // CH
TPC = CH // P
BPC = CH // S
PAIRS = NH // 2
PPH = PAIRS // KT
PM = NE * BOT // P
SG = BOT + NE
LN_EPS = 1e-5
SUM_EPS = 1e-8
SCORE_SCALE = 1.0 / float(np.sqrt(HD))
E_HI = float(np.exp(50.0))
E_LO = float(np.exp(-50.0))
RES_MAX = 0.3

C_BQ, C_BK, C_BD, C_BS, C_N = 0, KT, 2 * KT, 2 * KT + PM, 2 * KT + PM + 1


def xattn_moe(nc, x, ctx_t, mask_t, wq, wk, wv, wo, bv, bo, gamma, beta, rscale, vecs,
              wdn, wsg, wup, wsu, bu, bsu, ident_d, sel_d, out):
    f32 = mybir.dt.float32
    ALU = mybir.AluOpType
    ACT = mybir.ActivationFunctionType

    es = ExitStack()
    with es:
        def sb(name, shape, dt=f32):
            return es.enter_context(nc.sbuf_tensor(name, shape, dt))

        def sem(name):
            return es.enter_context(nc.semaphore(name))

        wq_sb, wk_sb, wo_sb = sb("wq_sb", [P, KT, H]), sb("wk_sb", [P, KT, H]), sb("wo_sb", [P, KT, H])
        wv_sb = sb("wv_sb", [P, KT, 2, P])
        bv_sb = sb("bv_sb", [P, P])
        bo_sb, gamma_sb, beta_sb = sb("bo_sb", [P, H]), sb("gamma_sb", [P, H]), sb("beta_sb", [P, H])
        vec_sb = sb("vec_sb", [P, C_N])
        wdn_sb = sb("wdn_sb", [P, KT, NE * BOT])
        wsg_sb = sb("wsg_sb", [P, KT, SG])
        wup_sb = sb("wup_sb", [P, PM, H])
        w5_sb = sb("w5_sb", [SG + 1, H])
        ident = sb("ident", [P, P])
        sel_sb = sb("sel_sb", [SG, PM, P])
        ones_bd = sb("ones_bd", [P, 32])
        neg_half, base_e = sb("neg_half", [P, TPC]), sb("base_e", [P, TPC])
        iota = sb("iota", [P, NE])
        mask_i = sb("mask_i", [P, B], mybir.dt.int32)
        mask_f = sb("mask_f", [P, B])
        e_cap = sb("e_cap", [P, B])
        rs_in, rs, rs2 = sb("rs_in", [P, 1]), sb("rs", [P, 1]), sb("rs2", [P, 1])

        x_sb = sb("x_sb", [P, NCH * TPC * H])
        y_sb = sb("y_sb", [P, NCH * TPC * H])
        ctx_sb = sb("ctx_sb", [P, KT, CH])
        st1, mv1 = sb("st1", [P, TPC, 6]), sb("mv1", [P, TPC, 2])
        ve1, rstd1 = sb("ve1", [P, TPC]), sb("rstd1", [P, TPC])
        nm1, nmr1 = sb("nm1", [P, TPC]), sb("nmr1", [P, TPC])
        h_sb = sb("h_sb", [P, TPC, H])
        ht_sb = sb("ht_sb", [P, KT, CH])
        qt_sb, kt_sb = sb("qt_sb", [P, KT, CH]), sb("kt_sb", [P, KT, CH])
        qbd = sb("qbd", [P, KT, 2, PPH, CH])
        vbd = sb("vbd", [P, BPC, PAIRS, 2, HD])
        e_sb = sb("e_sb", [P, 2, PAIRS * S])
        p_sb = sb("p_sb", [P, BPC, KT, PPH, S])
        rden = sb("rden", [P, KT * CH])
        ctxn = sb("ctxn", [P, KT, CH])
        t_sb, u_sb, xb_sb = sb("t_sb", [P, TPC, H]), sb("u_sb", [P, TPC, H]), sb("xb_sb", [P, TPC, H])
        sto, mvo = sb("sto", [P, TPC, 6]), sb("mvo", [P, TPC, 2])
        veo, pwo, coef = sb("veo", [P, TPC]), sb("pwo", [P, TPC]), sb("coef", [P, TPC])
        st2, mv2 = sb("st2", [P, TPC, 6]), sb("mv2", [P, TPC, 2])
        ve2, nm2 = sb("ve2", [P, TPC]), sb("nm2", [P, TPC])
        pw2 = sb("pw2", [P, TPC])
        rstd2, nmr2 = sb("rstd2", [P, NCH * TPC]), sb("nmr2", [P, NCH * TPC])

        h2_sb = sb("h2_sb", [P, TPC, H])
        h2t_sb = sb("h2t_sb", [P, KT, CH])
        g_sb, gc_sb = sb("g_sb", [P, PM, CH]), sb("gc_sb", [P, PM, CH])
        hs_sb = sb("hs_sb", [P, CH])
        lg_sb = sb("lg_sb", [SG, CH])
        lt_sb, m8 = sb("lt_sb", [P, TPC, NE]), sb("m8", [P, TPC, NE])
        i8 = sb("i8", [P, TPC, NE], mybir.dt.uint32)
        eq0, eq1 = sb("eq0", [P, TPC, NE]), sb("eq1", [P, TPC, NE])
        w0, w1 = sb("w0", [P, TPC, NE]), sb("w1", [P, TPC, NE])
        comb = sb("comb", [P, TPC, NE])
        dl, e2 = sb("dl", [P, TPC]), sb("e2", [P, TPC])
        s12, r1, r2 = sb("s12", [P, TPC]), sb("r1", [P, TPC]), sb("r2", [P, TPC])

        banks = [es.enter_context(nc.psum_tensor(f"bank{n}", [P, 512], f32)) for n in range(8)]
        b_t, b_q, b_k, b_s, b_pv, b_den, b_o = (banks[0], banks[1], banks[2], banks[3:5], banks[5],
                                                banks[6], banks[7])
        b_t2, b_sg, b_gt, b_d, b_bc, b_u = banks[0], banks[1], banks[2], banks[3:5], banks[5:7], banks[7]

        x0_in, x1_in, xr_in = sem("x0_in"), sem("x1_in"), sem("xr_in")
        ident_in, wq_in, wk_in, wv_in, vec_in = (sem("ident_in"), sem("wq_in"), sem("wk_in"),
                                                 sem("wv_in"), sem("vec_in"))
        mask_in, attn_w_in, ffn_w_in, iota_in = (sem("mask_in"), sem("attn_w_in"), sem("ffn_w_in"),
                                                 sem("iota_in"))
        ctx_in, qbd_in, stored = sem("ctx_in"), sem("qbd_in"), sem("stored")
        zeros_set, pool_const, ones_set, hs_ones, cap_set, rs_set = (
            sem("zeros_set"), sem("pool_const"), sem("ones_set"), sem("hs_ones"), sem("cap_set"),
            sem("rs_set"))
        stats1_raw, stats1, p_ve1, p_pw1, coef1 = (sem("stats1_raw"), sem("stats1"), sem("p_ve1"),
                                                   sem("p_pw1"), sem("coef1"))
        p_nm1, p_nm2 = sem("p_nm1"), sem("p_nm2")
        h_ready, t_psum, ht_ready = sem("h_ready"), sem("t_psum"), sem("ht_ready")
        q_psum, k_psum, v_psum = sem("q_psum"), sem("k_psum"), sem("v_psum")
        qt_ready, kt_ready, vbd_ready = sem("qt_ready"), sem("kt_ready"), sem("vbd_ready")
        s_psum, e_ready, p_ready = sem("s_psum"), sem("e_ready"), sem("p_ready")
        den_psum, rden_ready, ctxn_ready, o_psum = (sem("den_psum"), sem("rden_ready"),
                                                    sem("ctxn_ready"), sem("o_psum"))
        t_ready, statso_raw, statso = sem("t_ready"), sem("statso_raw"), sem("statso")
        p_veo, p_pwo, xb_ready, coef_o = sem("p_veo"), sem("p_pwo"), sem("xb_ready"), sem("coef_o")
        u_ready, y_ready, stats2_raw, stats2 = (sem("u_ready"), sem("y_ready"), sem("stats2_raw"),
                                                sem("stats2"))
        p_ve2, p_pw2, coef2 = sem("p_ve2"), sem("p_pw2"), sem("coef2")
        h2_ready, t2_psum, h2t_ready = sem("h2_ready"), sem("t2_psum"), sem("h2t_ready")
        sg_psum, lg_ready, lt_psum, lt_ready = (sem("sg_psum"), sem("lg_ready"), sem("lt_psum"),
                                                sem("lt_ready"))
        m8_ready, i8_ready, dl_ready, e2_ready, eq_ready = (sem("m8_ready"), sem("i8_ready"),
                                                            sem("dl_ready"), sem("e2_ready"),
                                                            sem("eq_ready"))
        s12_ready, r1_ready, r2_ready, w_ready, comb_ready = (sem("s12_ready"), sem("r1_ready"),
                                                              sem("r2_ready"), sem("w_ready"),
                                                              sem("comb_ready"))
        ct_psum, ct_ready, hs_ready = sem("ct_psum"), sem("ct_ready"), sem("hs_ready")
        d_psum, bc_psum, g_ready, gc_ready = sem("d_psum"), sem("bc_psum"), sem("g_ready"), sem("gc_ready")
        u_psum, out_ready = sem("u_psum"), sem("out_ready")

        def tile(buf, c, t):
            return buf[:, bass.ds((c * TPC + t) * H, H)]

        def chunk(buf, c):
            return buf[:, bass.ds(c * TPC * H, TPC * H)]

        def held(engine, value):
            return value if isinstance(value, int) else engine.snap(engine.to_reg(value))

        def wait_alone(engine, signal, value, passed):
            engine.wait_ge(passed, 1)
            engine.wait_ge(signal, value)

        block = es.enter_context(nc.Block())

        @block.sync
        def _(sp):
            def load_ctx(c):
                src = ctx_t[0] if isinstance(c, int) and c == 0 else ctx_t[bass.ds(c, 1)]
                if not (isinstance(c, int) and c == 0):
                    src = src.rearrange("a p k t -> (a p) k t")
                nc.sync.dma_start(ctx_sb[:, :, :], src).then_inc(ctx_in, 16)

            def spread_q(c):
                sp.wait_ge(qt_ready, c + 1)
                for par in range(2):
                    for j in range(PPH):
                        r = HD * (2 * j + par)
                        nc.sync.dma_start(qbd[r:r + HD, :, par, j, :],
                                          qt_sb[r:r + HD, :, :]).then_inc(qbd_in, 16)

            xv = x.rearrange("(n p) d -> p n d", p=P)
            xs = x_sb[:, :].rearrange("p (n d) -> p n d", d=H)
            nc.sync.dma_start(xs[:, 0:TPC], xv[:, 0:TPC]).then_inc(x0_in, 16)
            nc.sync.dma_start(ident[:, :], ident_d[:, 0:P]).then_inc(ident_in, 16)
            nc.sync.dma_start(wq_sb[:, :, :], wq).then_inc(wq_in, 16)
            load_ctx(0)
            nc.sync.dma_start(xs[:, TPC:2 * TPC], xv[:, TPC:2 * TPC]).then_inc(x1_in, 16)
            sp.wait_ge(zeros_set, 2)
            spread_q(0)
            nc.sync.dma_start(xs[:, 2 * TPC:], xv[:, 2 * TPC:]).then_inc(xr_in, 16)
            nc.sync.dma_start(iota[:, :], ident_d[:, P:P + NE]).then_inc(iota_in, 16)
            for dst, src in ((wdn_sb[:, :, :], wdn), (wsg_sb[:, :, :], wsg), (wup_sb[:, :, :], wup),
                             (w5_sb[0:BOT, :], wsu), (w5_sb[BOT:SG, :], bu), (w5_sb[SG:SG + 1, :], bsu),
                             (sel_sb[BOT:SG, :, :], sel_d)):
                nc.sync.dma_start(dst, src).then_inc(ffn_w_in, 16)

            with nc.sync.Fori(0, NCH - 1) as i:
                sp.wait_ge(v_psum, i + 1)
                load_ctx(i + 1)
                spread_q(i + 1)

            with nc.sync.Fori(0, NCH) as j:
                sp.wait_ge(out_ready, j + 1)
                nc.sync.dma_start(out[bass.ds(j * CH, CH), :].rearrange("(t p) d -> p t d", p=P),
                                  chunk(y_sb, j).rearrange("p (t d) -> p t d", d=H)).then_inc(stored, 16)
            sp.wait_ge(stored, 16 * NCH)

        @block.tensor
        def _(pe):
            def matmul(o, w, m, first=True, last=True):
                return nc.tensor.matmul(o, w, m, start=first, stop=last)

            def transpose_h(c):
                pe.wait_ge(h_ready, c + 1)
                for k in range(KT):
                    for t in range(TPC):
                        o = k * CH + t * P
                        done = nc.tensor.transpose(b_t[:, o:o + P], h_sb[:, t, k * P:(k + 1) * P],
                                                   ident[:, :])
                done.then_inc(t_psum, 1)

            def project(dst, w, m_sb, done_sem):
                for m in range(KT):
                    for k in range(KT):
                        done = matmul(dst[:, m * CH:(m + 1) * CH], w[:, k, m * P:(m + 1) * P],
                                      m_sb[:, k, :], k == 0, k == KT - 1)
                done.then_inc(done_sem, 1)

            def values(c):
                for b in range(BPC):
                    for k in range(KT):
                        for par in range(2):
                            done = matmul(b_t[S * par:S * par + S, b * P:(b + 1) * P],
                                          ctx_sb[:, k, b * S:(b + 1) * S], wv_sb[:, k, par, :],
                                          k == 0, k == KT - 1)
                done.then_inc(v_psum, 1)

            def scores(c, b):
                for hf in range(KT):
                    for par in range(2):
                        done = matmul(b_s[b % 2][S * par:S * par + S, hf * 256:(hf + 1) * 256],
                                      kt_sb[:, hf, b * S:(b + 1) * S],
                                      qbd[:, hf, par, :, b * S:(b + 1) * S])
                done.then_inc(s_psum, 1)

            def weigh(c, b):
                pe.wait_ge(p_ready, BPC * c + b + 1)
                for hf in range(KT):
                    for j in range(PPH):
                        matmul(b_pv[32 * j:32 * j + 32, (hf * BPC + b) * S:(hf * BPC + b + 1) * S],
                               vbd[:, b, hf * PPH + j, :, :], p_sb[:, b, hf, j, :])

            def denominators(c):
                for j in range(PPH):
                    for hf in range(KT):
                        done = matmul(b_den[32 * j:32 * j + 32, hf * CH:(hf + 1) * CH], ones_bd[:, :],
                                      p_sb[:, :, hf, j, :])
                done.then_inc(den_psum, 1)

            def project_out(c):
                pe.wait_ge(ctxn_ready, c + 1)
                for t in range(TPC):
                    for k in range(KT):
                        done = matmul(b_o[:, t * H:(t + 1) * H], ctxn[:, k, t * P:(t + 1) * P],
                                      wo_sb[:, k, :], k == 0, k == KT - 1)
                done.then_inc(o_psum, 1)

            def queries(c):
                pe.wait_ge(ht_ready, c + 1)
                project(b_q, wq_sb, ht_sb, q_psum)

            def keys_values(c):
                pe.wait_ge(ctx_in, 16 * (c + 1))
                project(b_k, wk_sb, ctx_sb, k_psum)
                values(c)

            def attend(c, prev, nxt):
                pe.wait_ge(qbd_in, 16 * 2 * PPH * (c + 1))
                pe.wait_ge(kt_ready, c + 1)
                scores(c, 0)
                scores(c, 1)
                if prev:
                    project_out(c - 1)
                pe.wait_ge(vbd_ready, c + 1)
                weigh(c, 0)
                if nxt:
                    transpose_h(c + 1)
                scores(c, 2)
                weigh(c, 1)
                scores(c, 3)
                if nxt:
                    queries(c + 1)
                weigh(c, 2)
                weigh(c, 3)
                denominators(c)
                if nxt:
                    keys_values(c + 1)

            def transpose_h2(c):
                pe.wait_ge(h2_ready, c + 1)
                for k in range(KT):
                    for t in range(TPC):
                        o = k * CH + t * P
                        done = nc.tensor.transpose(b_t2[:, o:o + P], h2_sb[:, t, k * P:(k + 1) * P],
                                                   ident[:, :])
                done.then_inc(t2_psum, 1)

            def shared_and_gates(c):
                pe.wait_ge(h2t_ready, c + 1)
                for k in range(KT):
                    done = matmul(b_sg[0:SG, 0:CH], wsg_sb[:, k, :], h2t_sb[:, k, :], k == 0, k == KT - 1)
                done.then_inc(sg_psum, 1)

            def logits_to_tokens(c):
                wait_alone(pe, lg_ready, c + 1, t_psum)
                for t in range(TPC):
                    done = nc.tensor.transpose(b_gt[:, CH + t * NE:CH + (t + 1) * NE],
                                               lg_sb[BOT:SG, t * P:(t + 1) * P], ident[BOT:SG, BOT:SG])
                done.then_inc(lt_psum, 1)

            def combine_to_rows(c):
                pe.wait_ge(comb_ready, c + 1)
                for t in range(TPC):
                    done = nc.tensor.transpose(b_gt[0:NE, t * P:(t + 1) * P], comb[:, t, :], ident[:, :])
                done.then_inc(ct_psum, 1)

            def down(c, half):
                for q in range(2):
                    m = 2 * half + q
                    for k in range(KT):
                        done = matmul(b_d[half][:, q * CH:(q + 1) * CH], wdn_sb[:, k, m * P:(m + 1) * P],
                                      h2t_sb[:, k, :], k == 0, k == KT - 1)
                done.then_inc(d_psum, 1)

            def broadcast_combine(c):
                pe.wait_ge(ct_ready, c + 1)
                for half in range(2):
                    for q in range(2):
                        done = matmul(b_bc[half][:, q * CH:(q + 1) * CH], sel_sb[BOT:SG, 2 * half + q, :],
                                      hs_sb[BOT:SG, :])
                    done.then_inc(bc_psum, 1)

            def up(c, t):
                tok = slice(t * P, (t + 1) * P)
                matmul(b_u[:, t * H:(t + 1) * H], hs_sb[0:SG + 1, tok], w5_sb[:, :], True, False)
                for m in range(PM):
                    if t == 0 and m % 2 == 0:
                        pe.wait_ge(gc_ready, 2 * c + m // 2 + 1)
                    done = matmul(b_u[:, t * H:(t + 1) * H], gc_sb[:, m, tok], wup_sb[:, m, :],
                                  False, m == PM - 1)
                return done

            def mix(c, prev, nxt):
                down(c, 0)
                combine_to_rows(c)
                if nxt:
                    transpose_h2(c + 1)
                down(c, 1)
                broadcast_combine(c)
                pe.wait_ge(hs_ready, c + 1)
                if nxt:
                    shared_and_gates(c + 1)
                if prev:
                    pe.wait_ge(out_ready, c)
                up(c, 0)
                if nxt:
                    logits_to_tokens(c + 1)
                up(c, 1).then_inc(u_psum, 1)

            pe.wait_ge(ident_in, 16)
            transpose_h(0)
            pe.wait_ge(wq_in, 16)
            queries(0)
            pe.wait_ge(wk_in, 16)
            pe.wait_ge(wv_in, 16)
            keys_values(0)
            pe.wait_ge(ones_set, 2)
            attend(0, False, True)
            pe.wait_ge(attn_w_in, 16 * 4)
            with nc.tensor.Fori(1, NCH - 1) as i:
                attend(i, True, True)
            attend(NCH - 1, True, False)
            pe.wait_ge(ffn_w_in, 16 * 7)
            transpose_h2(0)
            shared_and_gates(0)
            logits_to_tokens(0)
            project_out(NCH - 1)
            pe.wait_ge(y_ready, NCH)
            mix(0, False, True)
            with nc.tensor.Fori(1, NCH - 1) as j:
                mix(j, True, True)
            mix(NCH - 1, True, False)

        @block.scalar
        def _(act):
            def normalise(c):
                act.wait_ge(coef1, c + 1)
                for t in range(TPC):
                    done = nc.scalar.activation(h_sb[:, t, :], tile(x_sb, c, t), ACT.Identity,
                                                bias=nmr1[:, t:t + 1], scale=rstd1[:, t:t + 1])
                done.then_inc(h_ready, 1)

            def take_ht(c):
                act.wait_ge(t_psum, c + 1)
                nc.scalar.activation(ht_sb[:, :, :].rearrange("p k t -> p (k t)"), b_t[:, :],
                                     ACT.Copy).then_inc(ht_ready, 1)

            def take_qk(c):
                act.wait_ge(q_psum, c + 1)
                for m in range(KT):
                    done = nc.scalar.activation(qt_sb[:, m, :], b_q[:, m * CH:(m + 1) * CH], ACT.Identity,
                                                bias=vec_sb[:, C_BQ + m:C_BQ + m + 1])
                done.then_inc(qt_ready, 1)
                act.wait_ge(k_psum, c + 1)
                for m in range(KT):
                    done = nc.scalar.activation(kt_sb[:, m, :], b_k[:, m * CH:(m + 1) * CH], ACT.Identity,
                                                bias=vec_sb[:, C_BK + m:C_BK + m + 1])
                done.then_inc(kt_ready, 1)

            def exp(c, b):
                act.wait_ge(s_psum, BPC * c + b + 1)
                nc.scalar.activation(e_sb[:, b % 2, :], b_s[b % 2][:, :], ACT.Exp,
                                     scale=SCORE_SCALE).then_inc(e_ready, 1)

            def attend(c, nxt):
                exp(c, 0)
                exp(c, 1)
                if nxt:
                    normalise(c + 1)
                    take_ht(c + 1)
                exp(c, 2)
                exp(c, 3)
                if nxt:
                    take_qk(c + 1)

            def normalise2(c):
                act.wait_ge(coef2, c + 1)
                for t in range(TPC):
                    done = nc.scalar.activation(h2_sb[:, t, :], tile(y_sb, c, t), ACT.Identity,
                                                bias=nmr2[:, bass.ds(c * TPC + t, 1)],
                                                scale=rstd2[:, bass.ds(c * TPC + t, 1)])
                done.then_inc(h2_ready, 1)

            def take_h2t(c):
                act.wait_ge(t2_psum, c + 1)
                nc.scalar.activation(h2t_sb[:, :, :].rearrange("p k t -> p (k t)"), b_t2[:, :],
                                     ACT.Copy).then_inc(h2t_ready, 1)

            def gelu_shared(c):
                act.wait_ge(sg_psum, c + 1)
                nc.scalar.activation(hs_sb[0:BOT, :], b_sg[0:BOT, 0:CH], ACT.Gelu,
                                     bias=vec_sb[0:BOT, C_BS:C_BS + 1]).then_inc(hs_ready, 1)

            def gelu(c, half):
                act.wait_ge(d_psum, 2 * c + half + 1)
                for q in range(2):
                    m = 2 * half + q
                    done = nc.scalar.activation(g_sb[:, m, :], b_d[half][:, q * CH:(q + 1) * CH], ACT.Gelu,
                                                bias=vec_sb[:, C_BD + m:C_BD + m + 1])
                done.then_inc(g_ready, 1)

            def mix(c, nxt):
                if nxt:
                    normalise2(c + 1)
                gelu(c, 0)
                gelu(c, 1)
                if nxt:
                    take_h2t(c + 1)
                    act.wait_ge(u_psum, c + 1)
                    gelu_shared(c + 1)

            nc.scalar.dma_start(vec_sb[:, :], vecs).then_inc(vec_in, 16)
            nc.scalar.dma_start(wk_sb[:, :, :], wk).then_inc(wk_in, 16)
            nc.scalar.dma_start(wv_sb[:, :, :, :], wv).then_inc(wv_in, 16)
            nc.scalar.dma_start(bv_sb[0:S, :], bv[0].partition_broadcast(S)).then_inc(mask_in, 16)
            nc.scalar.dma_start(bv_sb[S:P, :], bv[1].partition_broadcast(S)).then_inc(mask_in, 16)
            nc.scalar.dma_start(mask_i[0:S, :], mask_t).then_inc(mask_in, 16)
            nc.scalar.dma_start(mask_i[S:P, :], mask_t).then_inc(mask_in, 16)
            nc.scalar.dma_start(rs_in[:, :], rscale.partition_broadcast(P)).then_inc(mask_in, 16)
            nc.scalar.dma_start(wo_sb[:, :, :], wo).then_inc(attn_w_in, 16)
            nc.scalar.dma_start(bo_sb[:, :], bo.partition_broadcast(P)).then_inc(attn_w_in, 16)
            nc.scalar.dma_start(gamma_sb[:, :], gamma.partition_broadcast(P)).then_inc(attn_w_in, 16)
            nc.scalar.dma_start(beta_sb[:, :], beta.partition_broadcast(P)).then_inc(attn_w_in, 16)
            normalise(0)
            take_ht(0)
            act.wait_ge(vec_in, 16)
            take_qk(0)
            with nc.scalar.Fori(0, NCH - 1) as i:
                attend(i, True)
            attend(NCH - 1, False)
            normalise2(0)
            take_h2t(0)
            act.wait_ge(hs_ones, 1)
            gelu_shared(0)
            with nc.scalar.Fori(0, NCH - 1) as j:
                mix(j, True)
            mix(NCH - 1, False)

        @block.vector
        def _(dve):
            V = nc.vector

            def stats_x(c, n):
                for t in range(TPC):
                    done = V.bn_stats(st1[:, t, :], tile(x_sb, c, t))
                done.then_inc(stats1_raw, 1)
                wait_alone(dve, stats1_raw, n, stats1_raw)
                for t in range(TPC):
                    done = V.bn_aggr(mv1[:, t, :], st1[:, t, :])
                done.then_inc(stats1, 1)

            def cap(c, b):
                dve.wait_ge(e_ready, BPC * c + b + 1)
                V.tensor_scalar(p_sb[:, b, :, :, :].rearrange("p h j s -> p (h j s)"), e_sb[:, b % 2, :],
                                e_cap[:, bass.ds(c * BPC + b, 1)], E_LO, ALU.min,
                                ALU.max).then_inc(p_ready, 1)

            def take_v(c):
                dve.wait_ge(v_psum, c + 1)
                for par in range(2):
                    r = slice(S * par, S * par + S)
                    done = V.tensor_tensor(
                        vbd[r, :, :, par, :],
                        b_t[r, :].rearrange("p (b q d) -> p b q d", b=BPC, d=HD),
                        bv_sb[r, :].rearrange("p (q d) -> p q d", d=HD).unsqueeze(1).broadcast_to(
                            [S, BPC, PAIRS, HD]), ALU.add)
                done.then_inc(vbd_ready, 1)

            def divide(c):
                dve.wait_ge(den_psum, c + 1)
                V.reciprocal(rden[:, :], b_den[:, :]).then_inc(rden_ready, 1)
                dve.wait_ge(rden_ready, c + 1)
                V.tensor_tensor(ctxn[:, :, :].rearrange("p k t -> p (k t)"), b_pv[:, :], rden[:, :],
                                ALU.mult).then_inc(ctxn_ready, 1)

            def delta_stats(c):
                dve.wait_ge(o_psum, c + 1)
                V.tensor_tensor(t_sb[:, :, :], b_o[:, :].rearrange("p (t d) -> p t d", d=H),
                                bo_sb[:, :].unsqueeze(1).broadcast_to([P, TPC, H]),
                                ALU.add).then_inc(t_ready, 1)
                wait_alone(dve, t_ready, c + 1, stats1_raw)
                for t in range(TPC):
                    done = V.bn_stats(sto[:, t, :], t_sb[:, t, :])
                done.then_inc(statso_raw, 1)
                wait_alone(dve, statso_raw, c + 1, stats1_raw)
                for t in range(TPC):
                    done = V.bn_aggr(mvo[:, t, :], sto[:, t, :])
                done.then_inc(statso, 1)

            def add_delta(c):
                dve.wait_ge(statso, c + 1)
                for t in range(TPC):
                    done = V.scalar_tensor_tensor(u_sb[:, t, :], t_sb[:, t, :], mvo[:, t, 0:1],
                                                  gamma_sb[:, :], ALU.subtract, ALU.mult)
                done.then_inc(u_ready, 1)
                dve.wait_ge(u_ready, c + 1)
                dve.wait_ge(coef_o, c + 1)
                for t in range(TPC):
                    done = V.scalar_tensor_tensor(tile(y_sb, c, t), u_sb[:, t, :], coef[:, t:t + 1],
                                                  xb_sb[:, t, :], ALU.mult, ALU.add)
                done.then_inc(y_ready, 1)
                wait_alone(dve, y_ready, c + 1, stats1_raw)
                for t in range(TPC):
                    done = V.bn_stats(st2[:, t, :], tile(y_sb, c, t))
                done.then_inc(stats2_raw, 1)
                wait_alone(dve, stats2_raw, c + 1, stats1_raw)
                for t in range(TPC):
                    done = V.bn_aggr(mv2[:, t, :], st2[:, t, :])
                done.then_inc(stats2, 1)

            def attend(c, prev, nxt):
                if nxt:
                    stats_x(c + 1, held(dve, c + 2))
                cap(c, 0)
                cap(c, 1)
                if prev:
                    delta_stats(c - 1)
                cap(c, 2)
                cap(c, 3)
                if prev:
                    add_delta(c - 1)
                divide(c)
                if nxt:
                    take_v(c + 1)

            def take_logits(c):
                dve.wait_ge(sg_psum, c + 1)
                V.tensor_copy(lg_sb[BOT:SG, :], b_sg[BOT:SG, 0:CH]).then_inc(lg_ready, 1)

            def choose(c):
                dve.wait_ge(lt_psum, c + 1)
                V.tensor_copy(lt_sb[:, :, :].rearrange("p t e -> p (t e)"),
                              b_gt[:, CH:CH + TPC * NE]).then_inc(lt_ready, 1)
                wait_alone(dve, lt_ready, c + 1, stats1_raw)
                for t in range(TPC):
                    done = V.max(m8[:, t, :], lt_sb[:, t, :])
                done.then_inc(m8_ready, 1)
                dve.wait_ge(m8_ready, c + 1)
                V.tensor_tensor(dl[:, :].unsqueeze(2), m8[:, :, 1:2], m8[:, :, 0:1],
                                ALU.subtract).then_inc(dl_ready, 1)
                for t in range(TPC):
                    done = V.max_index(i8[:, t, :], m8[:, t, :], lt_sb[:, t, :])
                done.then_inc(i8_ready, 1)
                dve.wait_ge(i8_ready, c + 1)
                for n, eq in enumerate((eq0, eq1)):
                    done = V.tensor_tensor(eq[:, :, :], iota[:, :].unsqueeze(1).broadcast_to([P, TPC, NE]),
                                           i8[:, :, n:n + 1].broadcast_to([P, TPC, NE]), ALU.is_equal)
                done.then_inc(eq_ready, 1)

            def combine(c):
                dve.wait_ge(e2_ready, c + 1)
                V.tensor_scalar(s12[:, :], e2[:, :], 1.0, None, ALU.add).then_inc(s12_ready, 1)
                dve.wait_ge(s12_ready, c + 1)
                V.reciprocal(r1[:, :], s12[:, :]).then_inc(r1_ready, 1)
                dve.wait_ge(r1_ready, c + 1)
                V.tensor_tensor(r2[:, :], e2[:, :], r1[:, :], ALU.mult).then_inc(r2_ready, 1)
                dve.wait_ge(r2_ready, c + 1)
                dve.wait_ge(eq_ready, c + 1)
                V.tensor_tensor(w0[:, :, :], eq0[:, :, :], r1[:, :].unsqueeze(2).broadcast_to([P, TPC, NE]),
                                ALU.mult)
                V.tensor_tensor(w1[:, :, :], eq1[:, :, :], r2[:, :].unsqueeze(2).broadcast_to([P, TPC, NE]),
                                ALU.mult).then_inc(w_ready, 1)
                dve.wait_ge(w_ready, c + 1)
                V.tensor_tensor(comb[:, :, :], w0[:, :, :], w1[:, :, :], ALU.add).then_inc(comb_ready, 1)

            def mix(c, nxt):
                dve.wait_ge(ct_psum, c + 1)
                V.tensor_copy(hs_sb[BOT:SG, :], b_gt[0:NE, 0:CH]).then_inc(ct_ready, 1)
                for half in range(2):
                    dve.wait_ge(bc_psum, 2 * c + half + 1)
                    dve.wait_ge(g_ready, 2 * c + half + 1)
                    V.tensor_tensor(gc_sb[:, 2 * half:2 * half + 2, :].rearrange("p m t -> p (m t)"),
                                    g_sb[:, 2 * half:2 * half + 2, :].rearrange("p m t -> p (m t)"),
                                    b_bc[half][:, :], ALU.mult).then_inc(gc_ready, 1)
                if nxt:
                    take_logits(c + 1)
                    choose(c + 1)
                dve.wait_ge(u_psum, c + 1)
                V.tensor_tensor(chunk(y_sb, c), b_u[:, :], chunk(y_sb, c), ALU.add).then_inc(out_ready, 1)
                if nxt:
                    combine(c + 1)

            V.memset(qbd[:, 0, :, :, :], 0.0).then_inc(zeros_set, 1)
            dve.wait_ge(x0_in, 16)
            stats_x(0, 1)
            V.memset(qbd[:, 1, :, :, :], 0.0).then_inc(zeros_set, 1)
            V.memset(vbd[:, :, :, :, :], 0.0)
            V.memset(ones_bd[:, :], 0.0).then_inc(ones_set, 1)
            dve.wait_ge(ones_set, 1)
            for par in range(2):
                done = V.memset(ones_bd[S * par:S * par + S, HD * par:HD * par + HD], 1.0 + SUM_EPS)
            done.then_inc(ones_set, 1)
            V.memset(hs_sb[BOT:P, :], 1.0).then_inc(hs_ones, 1)
            dve.wait_ge(mask_in, 16 * 5)
            V.tensor_copy(mask_f[:, :], mask_i[:, :]).then_inc(cap_set, 1)
            V.tensor_scalar(rs[:, :], rs_in[:, :], 0.0, RES_MAX, ALU.max, ALU.min).then_inc(rs_set, 1)
            dve.wait_ge(cap_set, 1)
            V.tensor_scalar(mask_f[:, :], mask_f[:, :], 0.5, E_HI, ALU.is_gt, ALU.mult).then_inc(cap_set, 1)
            dve.wait_ge(rs_set, 1)
            V.tensor_tensor(rs2[:, :], rs[:, :], rs[:, :], ALU.mult).then_inc(rs_set, 1)
            dve.wait_ge(cap_set, 2)
            V.tensor_scalar(e_cap[:, :], mask_f[:, :], E_LO, None, ALU.max).then_inc(cap_set, 1)
            dve.wait_ge(hs_ones, 1)
            take_v(0)
            dve.wait_ge(x1_in, 16)
            dve.wait_ge(cap_set, 3)
            attend(0, False, True)
            dve.wait_ge(xr_in, 16)
            dve.wait_ge(attn_w_in, 16 * 4)
            with nc.vector.Fori(1, NCH - 1) as i:
                attend(i, True, True)
            attend(NCH - 1, True, False)
            take_logits(0)
            delta_stats(NCH - 1)
            add_delta(NCH - 1)
            dve.wait_ge(iota_in, 16)
            choose(0)
            combine(0)
            with nc.vector.Fori(0, NCH - 1) as j:
                mix(j, True)
            mix(NCH - 1, False)

        @block.gpsimd
        def _(pool):
            G = nc.gpsimd

            def coef_x(c, n):
                wait_alone(pool, stats1, n, pool_const)
                G.tensor_scalar(ve1[:, :].unsqueeze(2), mv1[:, :, 1:2], LN_EPS, 1.0, ALU.add,
                                ALU.mult).then_inc(p_ve1, 1)
                wait_alone(pool, p_ve1, n, pool_const)
                G.tensor_scalar(nm1[:, :].unsqueeze(2), mv1[:, :, 0:1], -1.0, 0.0, ALU.mult,
                                ALU.add).then_inc(p_nm1, 1)
                pool.wait_ge(p_nm1, c + 1)
                G.tensor_tensor(rstd1[:, :], ve1[:, :], neg_half[:, :], ALU.pow).then_inc(p_pw1, 1)
                pool.wait_ge(p_pw1, c + 1)
                G.tensor_tensor(nmr1[:, :], nm1[:, :], rstd1[:, :], ALU.mult).then_inc(coef1, 1)

            def x_plus_beta(c):
                G.tensor_tensor(xb_sb[:, :, :], chunk(x_sb, c).rearrange("p (t d) -> p t d", d=H),
                                beta_sb[:, :].unsqueeze(1).broadcast_to([P, TPC, H]),
                                ALU.add).then_inc(xb_ready, 1)

            def coef_delta(c):
                wait_alone(pool, xb_ready, c + 1, pool_const)
                pool.wait_ge(statso, c + 1)
                G.tensor_scalar(veo[:, :].unsqueeze(2), mvo[:, :, 1:2], rs2[:, 0:1], LN_EPS, ALU.mult,
                                ALU.add).then_inc(p_veo, 1)
                pool.wait_ge(p_veo, c + 1)
                G.tensor_tensor(pwo[:, :], veo[:, :], neg_half[:, :], ALU.pow).then_inc(p_pwo, 1)
                wait_alone(pool, p_pwo, c + 1, pool_const)
                G.tensor_scalar(coef[:, :], pwo[:, :], rs[:, 0:1], 0.0, ALU.mult, ALU.add).then_inc(coef_o, 1)

            def coef_y(c):
                wait_alone(pool, coef_o, c + 1, pool_const)
                pool.wait_ge(stats2, c + 1)
                G.tensor_scalar(ve2[:, :].unsqueeze(2), mv2[:, :, 1:2], LN_EPS, 1.0, ALU.add,
                                ALU.mult).then_inc(p_ve2, 1)
                wait_alone(pool, p_ve2, c + 1, pool_const)
                G.tensor_scalar(nm2[:, :].unsqueeze(2), mv2[:, :, 0:1], -1.0, 0.0, ALU.mult,
                                ALU.add).then_inc(p_nm2, 1)
                pool.wait_ge(p_nm2, c + 1)
                G.tensor_tensor(rstd2[:, bass.ds(c * TPC, TPC)], ve2[:, :], neg_half[:, :],
                                ALU.pow).then_inc(p_pw2, 1)
                pool.wait_ge(p_pw2, c + 1)
                G.tensor_tensor(nmr2[:, bass.ds(c * TPC, TPC)], nm2[:, :], rstd2[:, bass.ds(c * TPC, TPC)],
                                ALU.mult).then_inc(coef2, 1)

            def attend(c, prev, nxt):
                if nxt:
                    coef_x(c + 1, held(pool, c + 2))
                    pool.wait_ge(coef1, c + 2)
                if prev:
                    deltas(c - 1)

            def deltas(c):
                x_plus_beta(c)
                coef_delta(c)
                coef_y(c)
                pool.wait_ge(coef2, c + 1)

            def exp_difference(c):
                pool.wait_ge(dl_ready, c + 1)
                G.tensor_tensor(e2[:, :], base_e[:, :], dl[:, :], ALU.pow).then_inc(e2_ready, 1)
                pool.wait_ge(e2_ready, c + 1)

            for n, (dst, value) in enumerate(((neg_half, -0.5), (base_e, float(np.e)))):
                G.memset(dst[:, :], value).then_inc(pool_const, 1)
                pool.wait_ge(pool_const, n + 1)
            coef_x(0, 1)
            pool.wait_ge(coef1, 1)
            attend(0, False, True)
            pool.wait_ge(xr_in, 16)
            pool.wait_ge(attn_w_in, 16 * 4)
            pool.wait_ge(rs_set, 2)
            with nc.gpsimd.Fori(1, NCH - 1) as i:
                attend(i, True, True)
            attend(NCH - 1, True, False)
            deltas(NCH - 1)
            with nc.gpsimd.Fori(0, NCH) as j:
                exp_difference(j)


_ORDER = ["x", "ctx_t", "mask_t", "wq", "wk", "wv", "wo", "bv", "bo", "gamma", "beta", "rscale", "vecs",
          "wdn", "wsg", "wup", "wsu", "bu", "bsu", "ident_d", "sel_d"]


def _layout(i):
    def rows(w, n):
        return w.T.reshape(-1, P, n).transpose(1, 0, 2)

    a = {k: np.asarray(v) for k, v in i.items()}
    d = {}
    d["x"] = a["x"].reshape(TOK, H)
    d["ctx_t"] = a["ctx_2048"].reshape(NCH, CH, KT, P).transpose(0, 3, 2, 1)
    d["mask_t"] = a["mask_BxS2_ik0"].T
    for n in "qko":
        d["w" + n] = rows(a["L0_xattn_W" + n], H)
    wv = rows(a["L0_xattn_Wv"], H).reshape(P, KT, PAIRS, 2, HD)
    d["wv"] = wv.transpose(0, 1, 3, 2, 4).reshape(P, KT, 2, P)
    d["bv"] = a["L0_xattn_bv"].reshape(PAIRS, 2, HD).transpose(1, 0, 2).reshape(2, P)
    d["bo"], d["gamma"], d["beta"] = a["L0_xattn_bo"], a["L0_xattn_ln_gamma"], a["L0_xattn_ln_beta"]
    d["rscale"] = a["L0_xattn_residual_scale"].reshape(1)
    bs = a["L0_ffn_bs_d"]
    d["vecs"] = np.concatenate([a["L0_xattn_bq"].reshape(KT, P), a["L0_xattn_bk"].reshape(KT, P),
                                a["L0_ffn_bd"].reshape(PM, P), np.concatenate([bs, bs])[None]]).T
    d["wdn"] = rows(a["L0_ffn_wd"].reshape(NE * BOT, H), NE * BOT)
    d["wsg"] = rows(np.concatenate([a["L0_ffn_ws_d"], a["L0_ffn_gate_w"]]), SG)
    d["wup"] = a["L0_ffn_wu"].transpose(0, 2, 1).reshape(PM, P, H).transpose(1, 0, 2)
    d["wsu"] = a["L0_ffn_ws_u"].T
    d["bu"] = a["L0_ffn_bu"]
    d["bsu"] = a["L0_ffn_bs_u"].reshape(1, H)
    d["ident_d"] = np.concatenate([np.eye(P, dtype=np.float32),
                                   np.tile(np.arange(NE, dtype=np.float32), (P, 1))], axis=1)
    sel = np.zeros((NE, PM, P), np.float32)
    for e in range(NE):
        sel[e, e // 2, BOT * (e % 2):BOT * (e % 2) + BOT] = 1.0
    d["sel_d"] = sel
    return {k: np.ascontiguousarray(v) for k, v in d.items()}


def kernel(**inputs):
    import concourse.bacc as bacc
    from concourse.bass_utils import run_bass_kernel_spmd

    nc = bacc.Bacc("TRN2", target_bir_lowering=False, num_devices=1)
    data = _layout(inputs)
    arrays, args = {}, []
    for name in _ORDER:
        arrays[f"in_{name}"] = data[name]
        args.append(nc.dram_tensor(f"in_{name}", data[name].shape, mybir.dt.from_np(data[name].dtype),
                                   kind="ExternalInput").ap())
    args.append(nc.dram_tensor("out_y", (TOK, H), mybir.dt.float32, kind="ExternalOutput").ap())
    xattn_moe(nc, *args)
    r = run_bass_kernel_spmd(nc, [arrays], core_ids=[0])
    return r.results[0]["out_y"].reshape(B, S, H)
```

```python
import numpy as np
import concourse.bass as bass
from concourse import mybir
from contextlib import ExitStack

B, S, H = 32, 64, 256
NH, HD = 16, 16
NE, BOT = 8, 64
TOK = B * S

P = 128
KT = H // P
CH = 256
NCH = TOK // CH
TPC = CH // P
BPC = CH // S
PAIRS = NH // 2
PPH = PAIRS // KT
PM = NE * BOT // P
SG = BOT + NE
NP = 3
ONES = BOT + NP * NE
LN_EPS = 1e-5
SUM_EPS = 1e-8
SCORE_SCALE = 1.0 / float(np.sqrt(HD))
E_HI = float(np.exp(50.0))
E_LO = float(np.exp(-50.0))
RES_MAX = 0.3

C_BQ, C_BK, C_BV, C_BD, C_BS, C_N = 0, KT, 2 * KT, 3 * KT, 3 * KT + PM, 3 * KT + PM + 1


def xattn_moe(nc, x, ctx_t, mask_t, wq, wk, wv, wo, bo, gamma, beta, rscale, vecs,
              wdn, wsg, wup, w5, ident_d, sel_d, out):
    f32, bf16 = mybir.dt.float32, mybir.dt.bfloat16
    ALU = mybir.AluOpType
    ACT = mybir.ActivationFunctionType

    es = ExitStack()
    with es:
        def sb(name, shape, dt=f32):
            return es.enter_context(nc.sbuf_tensor(name, shape, dt))

        def sem(name):
            return es.enter_context(nc.semaphore(name))

        wq_sb, wk_sb, wo_sb = sb("wq_sb", [P, KT, H]), sb("wk_sb", [P, KT, H]), sb("wo_sb", [P, KT, H])
        wv_sb = sb("wv_sb", [P, KT, H])
        bo_sb, gamma_sb, beta_sb = sb("bo_sb", [P, H]), sb("gamma_sb", [P, H]), sb("beta_sb", [P, H])
        vec_sb = sb("vec_sb", [P, C_N])
        wdn_sb = sb("wdn_sb", [P, KT, NE * BOT])
        wsg_sb = sb("wsg_sb", [P, KT, SG])
        wup_sb = sb("wup_sb", [P, PM, H])
        w5_sb = sb("w5_sb", [ONES + 1, H])
        wobv_sb = sb("wobv_sb", [P, H])
        sel_f, sel_sb = sb("sel_f", [NP * NE, PM, P]), sb("sel_sb", [NP * NE, PM, P], bf16)
        ident_h = sb("ident_h", [P, P], bf16)
        ones_bd = sb("ones_bd", [P, 32])
        neg_half, base_e = sb("neg_half", [P, TPC]), sb("base_e", [P, TPC])
        const_sb = sb("const_sb", [P, P + NE + P // HD])
        ident, iota, head_of = const_sb[:, 0:P], const_sb[:, P:P + NE], const_sb[:, P + NE:]
        bq_head = sb("bq_head", [P, KT, P // HD])
        mask_i = sb("mask_i", [P, B], mybir.dt.int32)
        mask_f = sb("mask_f", [P, B])
        e_cap = sb("e_cap", [P, B])
        rs_in, rs, rs2 = sb("rs_in", [P, 1]), sb("rs", [P, 1]), sb("rs2", [P, 1])

        x_sb = sb("x_sb", [P, NCH * TPC * H])
        y_sb = sb("y_sb", [P, NCH * TPC * H])
        ctx_sb = sb("ctx_sb", [P, KT, CH])
        st1, mv1 = sb("st1", [P, TPC, 6]), sb("mv1", [P, TPC, 2])
        ve1, rstd1 = sb("ve1", [P, TPC]), sb("rstd1", [P, TPC])
        nm1, nmr1 = sb("nm1", [P, TPC]), sb("nmr1", [P, TPC])
        h_sb = sb("h_sb", [P, TPC, H])
        ht_sb = sb("ht_sb", [P, KT, CH])
        qt_sb, kt_sb = sb("qt_sb", [P, KT, CH]), sb("kt_sb", [P, KT, CH])
        qbd = sb("qbd", [P, 2, KT, 2, PPH, CH])
        vbd = sb("vbd", [P, BPC, PAIRS, 2, HD])
        e_sb = sb("e_sb", [P, 2, PAIRS * S])
        p_sb = sb("p_sb", [P, BPC, KT, PPH, S])
        rden = sb("rden", [P, KT * CH])
        ctxn = sb("ctxn", [P, KT, CH])
        u_sb = sb("u_sb", [P, TPC, H])
        sto, mvo = sb("sto", [P, TPC, 6]), sb("mvo", [P, TPC, 2])
        veo, pwo = sb("veo", [P, TPC]), sb("pwo", [P, TPC])
        mean_o, coef_d = sb("mean_o", [P, NCH * TPC]), sb("coef_d", [P, NCH * TPC])
        st2, mv2 = sb("st2", [P, TPC, 6]), sb("mv2", [P, TPC, 2])
        ve2, nm2 = sb("ve2", [P, TPC]), sb("nm2", [P, TPC])
        rstd2, nmr2 = sb("rstd2", [P, NCH * TPC]), sb("nmr2", [P, NCH * TPC])

        h2_sb = sb("h2_sb", [P, TPC, H])
        h2t_sb = sb("h2t_sb", [P, 2, KT, CH])
        g_sb, gc_sb = sb("g_sb", [P, PM, CH]), sb("gc_sb", [P, PM, CH])
        hs_sb = sb("hs_sb", [P, 2, CH])
        lg_sb = sb("lg_sb", [SG, CH])
        lt_sb, m8 = sb("lt_sb", [P, TPC, NE]), sb("m8", [P, TPC, NE])
        i8 = sb("i8", [P, TPC, NE], mybir.dt.uint32)
        eq0, eq1 = sb("eq0", [P, TPC, NE]), sb("eq1", [P, TPC, NE])
        w0, w1 = sb("w0", [P, TPC, NE]), sb("w1", [P, TPC, NE])
        comb, rest = sb("comb", [P, TPC, NE]), sb("rest", [P, TPC, NE])
        parts = sb("parts", [P, TPC, NP, NE], bf16)
        cr_sb = sb("cr_sb", [NP * NE, CH], bf16)
        dl, e2 = sb("dl", [P, TPC]), sb("e2", [P, TPC])
        s12, r1, r2 = sb("s12", [P, TPC]), sb("r1", [P, TPC]), sb("r2", [P, TPC])

        banks = [es.enter_context(nc.psum_tensor(f"bank{n}", [P, 512], f32)) for n in range(8)]
        b_t, b_q, b_k, b_s, b_pv, b_den, b_o = (banks[0], banks[1], banks[2], banks[3:5], banks[5],
                                                banks[6], banks[7])
        b_q0 = (banks[6], banks[5])
        b_t2, b_sg, b_gt, b_d, b_bc, b_u = banks[0], banks[1], banks[2], banks[3:5], banks[5:7], banks[7]

        b_ct = b_gt[0:NP * NE, 0:CH // 2].bitcast(bf16)

        x0_in, x1_in, x23_in, xr_in = sem("x0_in"), sem("x1_in"), sem("x23_in"), sem("xr_in")
        ident_in, wq_in, wk_in, wv_in, vec_in = (sem("ident_in"), sem("wq_in"), sem("wk_in"),
                                                 sem("wv_in"), sem("vec_in"))
        mask_in, attn_w_in, ffn_w_in = sem("mask_in"), sem("attn_w_in"), sem("ffn_w_in")
        bq_head_ready, q0_ready = sem("bq_head_ready"), sem("q0_ready")
        ctx_in, qbd_in, stored = sem("ctx_in"), sem("qbd_in"), sem("stored")
        zeros_set, pool_const, ones_set, hs_ones, vbd_zeros, cap_set, rs_set = (
            sem("zeros_set"), sem("pool_const"), sem("ones_set"), sem("hs_ones"), sem("vbd_zeros"), sem("cap_set"),
            sem("rs_set"))
        stats1_raw, stats1, p_ve1, p_pw1, coef1 = (sem("stats1_raw"), sem("stats1"), sem("p_ve1"),
                                                   sem("p_pw1"), sem("coef1"))
        p_nm1, p_nm2, mvo_free = sem("p_nm1"), sem("p_nm2"), sem("mvo_free")
        bias_psum, bias_ready = sem("bias_psum"), sem("bias_ready")
        h_ready, t_psum, ht_ready = sem("h_ready"), sem("t_psum"), sem("ht_ready")
        q_psum, k_psum, v_psum = sem("q_psum"), sem("k_psum"), sem("v_psum")
        q_psum0 = (sem("q_psum0_a"), sem("q_psum0_b"))
        qt_ready, kt_ready, vbd_ready = sem("qt_ready"), sem("kt_ready"), sem("vbd_ready")
        s_psum, e_ready, p_ready = sem("s_psum"), sem("e_ready"), sem("p_ready")
        den_psum, rden_ready, ctxn_ready, o_psum = (sem("den_psum"), sem("rden_ready"),
                                                    sem("ctxn_ready"), sem("o_psum"))
        t_ready, statso_raw, statso = sem("t_ready"), sem("statso_raw"), sem("statso")
        p_veo, p_pwo, xb_ready, coef_o = sem("p_veo"), sem("p_pwo"), sem("xb_ready"), sem("coef_o")
        u_ready, y_ready, stats2_raw, stats2 = (sem("u_ready"), sem("y_ready"), sem("stats2_raw"),
                                                sem("stats2"))
        p_ve2, p_pw2, coef2 = sem("p_ve2"), sem("p_pw2"), sem("coef2")
        h2_ready, t2_psum, h2t_ready = sem("h2_ready"), sem("t2_psum"), sem("h2t_ready")
        sg_psum, lg_ready, lt_psum, lt_ready = (sem("sg_psum"), sem("lg_ready"), sem("lt_psum"),
                                                sem("lt_ready"))
        m8_ready, i8_ready, dl_ready, e2_ready, eq_ready = (sem("m8_ready"), sem("i8_ready"),
                                                            sem("dl_ready"), sem("e2_ready"),
                                                            sem("eq_ready"))
        s12_ready, r1_ready, r2_ready, w_ready, comb_ready = (sem("s12_ready"), sem("r1_ready"),
                                                              sem("r2_ready"), sem("w_ready"),
                                                              sem("comb_ready"))
        ct_psum, ct_ready, hs_ready = sem("ct_psum"), sem("ct_ready"), sem("hs_ready")
        sel_ready, rest_ready = sem("sel_ready"), sem("rest_ready")
        d_psum, bc_psum, g_ready, gc_ready = sem("d_psum"), sem("bc_psum"), sem("g_ready"), sem("gc_ready")
        u_psum, out_ready = sem("u_psum"), sem("out_ready")

        def tile(buf, c, t):
            return buf[:, bass.ds((c * TPC + t) * H, H)]

        def chunk(buf, c):
            return buf[:, bass.ds(c * TPC * H, TPC * H)]

        def held(engine, value):
            return value if isinstance(value, int) else engine.snap(engine.to_reg(value))

        def wait_alone(engine, signal, value, passed):
            engine.wait_ge(passed, 1)
            engine.wait_ge(signal, value)

        block = es.enter_context(nc.Block())

        @block.sync
        def _(sp):
            def load_ctx(c):
                src = ctx_t[0] if isinstance(c, int) and c == 0 else ctx_t[bass.ds(c, 1)]
                if not (isinstance(c, int) and c == 0):
                    src = src.rearrange("a p k t -> (a p) k t")
                nc.sync.dma_start(ctx_sb[:, :, :], src).then_inc(ctx_in, 16)

            def spread_q(c, slot):
                sp.wait_ge(qt_ready, c)
                for par in range(2):
                    for j in range(PPH):
                        r = HD * (2 * j + par)
                        nc.sync.dma_start(qbd[r:r + HD, slot, :, par, j, :],
                                          qt_sb[r:r + HD, :, :]).then_inc(qbd_in, 16)

            xv = x.rearrange("(n p) d -> p n d", p=P)
            xs = x_sb[:, :].rearrange("p (n d) -> p n d", d=H)
            nc.sync.dma_start(xs[:, 0:TPC], xv[:, 0:TPC]).then_inc(x0_in, 16)
            load_ctx(0)
            nc.sync.dma_start(const_sb[:, :], ident_d).then_inc(ident_in, 16)
            nc.sync.dma_start(wq_sb[:, :, :], wq).then_inc(wq_in, 16)
            nc.sync.dma_start(xs[:, TPC:2 * TPC], xv[:, TPC:2 * TPC]).then_inc(x1_in, 16)
            for dst, src in ((wo_sb[:, :, :], wo), (bo_sb[:, :], bo.partition_broadcast(P)),
                             (gamma_sb[:, :], gamma.partition_broadcast(P)),
                             (beta_sb[:, :], beta.partition_broadcast(P))):
                nc.sync.dma_start(dst, src).then_inc(attn_w_in, 16)
            for dst, src in ((mask_i[0:S, :], mask_t), (mask_i[S:P, :], mask_t),
                             (rs_in[:, :], rscale.partition_broadcast(P))):
                nc.sync.dma_start(dst, src).then_inc(mask_in, 16)
            nc.sync.dma_start(xs[:, 2 * TPC:4 * TPC], xv[:, 2 * TPC:4 * TPC]).then_inc(x23_in, 16)
            nc.sync.dma_start(xs[:, 4 * TPC:], xv[:, 4 * TPC:]).then_inc(xr_in, 16)
            for dst, src in ((wdn_sb[:, :, :], wdn), (wsg_sb[:, :, :], wsg), (wup_sb[:, :, :], wup),
                             (w5_sb[:, :], w5), (sel_f[:, :, :], sel_d)):
                nc.sync.dma_start(dst, src).then_inc(ffn_w_in, 16)

            def prepare(c, slot):
                sp.wait_ge(v_psum, c)
                load_ctx(c)
                spread_q(c, slot)

            sp.wait_ge(zeros_set, 1)
            with nc.sync.Fori(1, NCH - 1, 2) as i:
                prepare(i, 1)
                prepare(i + 1, 0)
            prepare(NCH - 1, 1)

            with nc.sync.Fori(0, NCH) as j:
                sp.wait_ge(out_ready, j + 1)
                nc.sync.dma_start(out[bass.ds(j * CH, CH), :].rearrange("(t p) d -> p t d", p=P),
                                  chunk(y_sb, j).rearrange("p (t d) -> p t d", d=H)).then_inc(stored, 16)
            sp.wait_ge(stored, 16 * NCH)

        @block.tensor
        def _(pe):
            def matmul(o, w, m, first=True, last=True):
                return nc.tensor.matmul(o, w, m, start=first, stop=last)

            def transpose_h(c):
                pe.wait_ge(h_ready, c + 1)
                for k in range(KT):
                    for t in range(TPC):
                        o = k * CH + t * P
                        done = nc.tensor.transpose(b_t[:, o:o + P], h_sb[:, t, k * P:(k + 1) * P],
                                                   ident)
                done.then_inc(t_psum, 1)

            def project(dst, w, m_sb, done_sem):
                for m in range(KT):
                    for k in range(KT):
                        done = matmul(dst[:, m * CH:(m + 1) * CH], w[:, k, m * P:(m + 1) * P],
                                      m_sb[:, k, :], k == 0, k == KT - 1)
                done.then_inc(done_sem, 1)

            def values(c, first=False):
                if not first:
                    pe.wait_ge(qt_ready, c)
                for g in range(BPC // 2):
                    for k in range(KT):
                        done = matmul(b_q[:, g * H:(g + 1) * H], ctx_sb[:, k, g * P:(g + 1) * P],
                                      wv_sb[:, k, :], k == 0, k == KT - 1)
                done.then_inc(v_psum, 1)

            def scores(b, slot):
                for hf in range(KT):
                    for par in range(2):
                        done = matmul(b_s[b % 2][S * par:S * par + S, hf * 256:(hf + 1) * 256],
                                      kt_sb[:, hf, b * S:(b + 1) * S],
                                      qbd[:, slot, hf, par, :, b * S:(b + 1) * S])
                done.then_inc(s_psum, 1)

            def weigh(c, b):
                pe.wait_ge(p_ready, BPC * c + b + 1)
                for hf in range(KT):
                    for j in range(PPH):
                        matmul(b_pv[32 * j:32 * j + 32, (hf * BPC + b) * S:(hf * BPC + b + 1) * S],
                               vbd[:, b, hf * PPH + j, :, :], p_sb[:, b, hf, j, :])

            def denominators(c):
                for j in range(PPH):
                    for hf in range(KT):
                        done = matmul(b_den[32 * j:32 * j + 32, hf * CH:(hf + 1) * CH], ones_bd[:, :],
                                      p_sb[:, :, hf, j, :])
                done.then_inc(den_psum, 1)

            def project_out(c):
                pe.wait_ge(ctxn_ready, c + 1)
                for t in range(TPC):
                    for k in range(KT):
                        done = matmul(b_o[:, t * H:(t + 1) * H], ctxn[:, k, t * P:(t + 1) * P],
                                      wo_sb[:, k, :], k == 0, k == KT - 1)
                done.then_inc(o_psum, 1)

            def queries(c):
                pe.wait_ge(vbd_ready, c)
                pe.wait_ge(ht_ready, c + 1)
                project(b_q, wq_sb, ht_sb, q_psum)

            def first_queries():
                pe.wait_ge(ht_ready, 1)
                for m in range(KT):
                    for k in range(KT):
                        done = matmul(b_q0[m][:, 0:CH], wq_sb[:, k, m * P:(m + 1) * P], ht_sb[:, k, :],
                                      k == 0, k == KT - 1)
                    done.then_inc(q_psum0[m], 1)

            def keys(c):
                pe.wait_ge(ctx_in, 16 * (c + 1))
                project(b_k, wk_sb, ctx_sb, k_psum)

            def attend(c, slot, prev, nxt):
                if prev:
                    pe.wait_ge(qbd_in, 16 * 2 * PPH * c)
                else:
                    pe.wait_ge(q0_ready, 2)
                pe.wait_ge(kt_ready, c + 1)
                scores(0, slot)
                if nxt:
                    transpose_h(c + 1)
                scores(1, slot)
                if nxt:
                    queries(c + 1)
                if not nxt:
                    transpose_h2(0)
                if prev:
                    project_out(c - 1)
                pe.wait_ge(vbd_ready, c + 1)
                weigh(c, 0)
                scores(2, slot)
                if not nxt:
                    shared_and_gates(0, 0)
                weigh(c, 1)
                scores(3, slot)
                if nxt:
                    keys(c + 1)
                weigh(c, 2)
                if not nxt:
                    logits_to_tokens(0)
                weigh(c, 3)
                denominators(c)
                if nxt:
                    values(c + 1)

            def bias_through_wo():
                for k in range(KT):
                    done = matmul(b_o[:, 0:H], vec_sb[:, C_BV + k:C_BV + k + 1].broadcast_to([P, P]),
                                  wo_sb[:, k, :], k == 0, k == KT - 1)
                done.then_inc(bias_psum, 1)

            def transpose_h2(c):
                pe.wait_ge(h2_ready, c + 1)
                for k in range(KT):
                    for t in range(TPC):
                        o = k * CH + t * P
                        done = nc.tensor.transpose(b_t2[:, o:o + P], h2_sb[:, t, k * P:(k + 1) * P],
                                                   ident)
                done.then_inc(t2_psum, 1)

            def shared_and_gates(c, slot):
                pe.wait_ge(h2t_ready, c + 1)
                for k in range(KT):
                    done = matmul(b_sg[0:SG, 0:CH], wsg_sb[:, k, :], h2t_sb[:, slot, k, :], k == 0,
                                  k == KT - 1)
                done.then_inc(sg_psum, 1)

            def logits_to_tokens(c):
                wait_alone(pe, lg_ready, c + 1, t_psum)
                for t in range(TPC):
                    done = nc.tensor.transpose(b_gt[:, CH + t * NE:CH + (t + 1) * NE],
                                               lg_sb[BOT:SG, t * P:(t + 1) * P], ident[BOT:SG, BOT:SG])
                done.then_inc(lt_psum, 1)

            def combine_to_rows(c):
                pe.wait_ge(comb_ready, c + 1)
                for t in range(TPC):
                    done = nc.tensor.transpose(b_ct[:, t * P:(t + 1) * P],
                                               parts[:, t, :, :].rearrange("p n e -> p (n e)"),
                                               ident_h[:, :])
                done.then_inc(ct_psum, 1)

            def down(c, half, slot):
                for q in range(2):
                    m = 2 * half + q
                    for k in range(KT):
                        done = matmul(b_d[half][:, q * CH:(q + 1) * CH], wdn_sb[:, k, m * P:(m + 1) * P],
                                      h2t_sb[:, slot, k, :], k == 0, k == KT - 1)
                done.then_inc(d_psum, 1)

            def broadcast_combine():
                for half in range(2):
                    for q in range(2):
                        done = matmul(b_bc[half][:, q * CH:(q + 1) * CH], sel_sb[:, 2 * half + q, :],
                                      cr_sb[:, :])
                    done.then_inc(bc_psum, 1)

            def up(c, t, slot):
                tok = slice(t * P, (t + 1) * P)
                matmul(b_u[:, t * H:(t + 1) * H], hs_sb[0:ONES + 1, slot, tok], w5_sb[:, :], True, False)
                for m in range(PM):
                    if t == 0 and m % 2 == 0:
                        pe.wait_ge(gc_ready, 2 * c + m // 2 + 1)
                    done = matmul(b_u[:, t * H:(t + 1) * H], gc_sb[:, m, tok], wup_sb[:, m, :],
                                  False, m == PM - 1)
                return done

            def mix(c, slot, prev, nxt):
                if nxt:
                    transpose_h2(c + 1)
                down(c, 0, slot)
                if prev:
                    combine_to_rows(c)
                down(c, 1, slot)
                if not prev:
                    pe.wait_ge(hs_ready, 1)
                    shared_and_gates(1, 1 - slot)
                    project_out(NCH - 1)
                    combine_to_rows(c)
                pe.wait_ge(ct_ready, c + 1)
                broadcast_combine()
                if prev and nxt:
                    pe.wait_ge(hs_ready, c + 1)
                    shared_and_gates(c + 1, 1 - slot)
                if prev:
                    pe.wait_ge(out_ready, c)
                else:
                    pe.wait_ge(t_ready, NCH)
                up(c, 0, slot)
                if nxt:
                    logits_to_tokens(c + 1)
                up(c, 1, slot).then_inc(u_psum, 1)

            pe.wait_ge(wk_in, 16)
            keys(0)
            pe.wait_ge(ident_in, 16)
            transpose_h(0)
            pe.wait_ge(wq_in, 16)
            first_queries()
            pe.wait_ge(ones_set, 2)
            pe.wait_ge(vec_in, 16)
            pe.wait_ge(attn_w_in, 16 * 4)
            bias_through_wo()
            pe.wait_ge(wv_in, 16)
            values(0, True)
            attend(0, 0, False, True)
            pe.wait_ge(bias_ready, 1)
            with nc.tensor.Fori(1, NCH - 1, 2) as i:
                attend(i, 1, True, True)
                attend(i + 1, 0, True, True)
            pe.wait_ge(ffn_w_in, 16 * 5)
            pe.wait_ge(sel_ready, 1)
            attend(NCH - 1, 1, True, False)
            mix(0, 0, False, True)
            with nc.tensor.Fori(1, NCH - 1, 2) as j:
                mix(j, 1, True, True)
                mix(j + 1, 0, True, True)
            mix(NCH - 1, 1, True, False)

        @block.scalar
        def _(act):
            def normalise(c):
                act.wait_ge(coef1, c + 1)
                for t in range(TPC):
                    done = nc.scalar.activation(h_sb[:, t, :], tile(x_sb, c, t), ACT.Identity,
                                                bias=nmr1[:, t:t + 1], scale=rstd1[:, t:t + 1])
                done.then_inc(h_ready, 1)

            def take_ht(c):
                act.wait_ge(t_psum, c + 1)
                nc.scalar.activation(ht_sb[:, :, :].rearrange("p k t -> p (k t)"), b_t[:, :],
                                     ACT.Copy).then_inc(ht_ready, 1)

            def take_q(c):
                act.wait_ge(q_psum, c)
                for m in range(KT):
                    done = nc.scalar.activation(qt_sb[:, m, :], b_q[:, m * CH:(m + 1) * CH], ACT.Identity,
                                                bias=vec_sb[:, C_BQ + m:C_BQ + m + 1])
                done.then_inc(qt_ready, 1)

            def take_k(c):
                act.wait_ge(k_psum, c + 1)
                for m in range(KT):
                    done = nc.scalar.activation(kt_sb[:, m, :], b_k[:, m * CH:(m + 1) * CH], ACT.Identity,
                                                bias=vec_sb[:, C_BK + m:C_BK + m + 1])
                done.then_inc(kt_ready, 1)

            def take_v(c):
                act.wait_ge(v_psum, c + 1)
                for n in range(2):
                    for par in range(2):
                        for g in range(BPC // 2):
                            src = b_q[S * n:S * n + S, g * H + par * P:g * H + par * P + P]
                            done = nc.scalar.activation(vbd[S * par:S * par + S, 2 * g + n, :, par, :],
                                                        src.rearrange("p (q d) -> p q d", d=HD), ACT.Copy)
                done.then_inc(vbd_ready, 1)

            def exp(c, b):
                act.wait_ge(s_psum, BPC * c + b + 1)
                nc.scalar.activation(e_sb[:, b % 2, :], b_s[b % 2][:, :], ACT.Exp,
                                     scale=SCORE_SCALE).then_inc(e_ready, 1)

            def attend(c, nxt, after):
                if nxt:
                    take_ht(c + 1)
                exp(c, 0)
                exp(c, 1)
                if nxt:
                    take_q(c + 1)
                if after:
                    normalise(c + 2)
                elif nxt:
                    normalise2(0)
                else:
                    take_h2t(0, 0)
                exp(c, 2)
                if not nxt:
                    take_logits(0)
                exp(c, 3)
                if not nxt:
                    normalise2(1)
                if nxt:
                    take_k(c + 1)
                    take_v(c + 1)

            def normalise2(c):
                act.wait_ge(coef2, c + 1)
                for t in range(TPC):
                    done = nc.scalar.activation(h2_sb[:, t, :], tile(y_sb, c, t), ACT.Identity,
                                                bias=nmr2[:, bass.ds(c * TPC + t, 1)],
                                                scale=rstd2[:, bass.ds(c * TPC + t, 1)])
                done.then_inc(h2_ready, 1)

            def take_h2t(c, slot):
                act.wait_ge(t2_psum, c + 1)
                nc.scalar.activation(h2t_sb[:, slot, :, :].rearrange("p k t -> p (k t)"), b_t2[:, :],
                                     ACT.Copy).then_inc(h2t_ready, 1)

            def gelu_shared(c, slot):
                act.wait_ge(sg_psum, c + 1)
                nc.scalar.activation(hs_sb[0:BOT, slot, :], b_sg[0:BOT, 0:CH], ACT.Gelu,
                                     bias=vec_sb[0:BOT, C_BS:C_BS + 1]).then_inc(hs_ready, 1)

            def take_logits(c):
                act.wait_ge(sg_psum, c + 1)
                nc.scalar.activation(lg_sb[BOT:SG, :], b_sg[BOT:SG, 0:CH], ACT.Copy).then_inc(lg_ready, 1)

            def take_combine(c, slot):
                act.wait_ge(ct_psum, c + 1)
                nc.scalar.activation(cr_sb[:, :], b_ct, ACT.Copy)
                nc.scalar.activation(hs_sb[BOT:ONES, slot, :], b_ct, ACT.Copy).then_inc(ct_ready, 1)

            def gelu(c, half):
                act.wait_ge(d_psum, 2 * c + half + 1)
                for q in range(2):
                    m = 2 * half + q
                    done = nc.scalar.activation(g_sb[:, m, :], b_d[half][:, q * CH:(q + 1) * CH], ACT.Gelu,
                                                bias=vec_sb[:, C_BD + m:C_BD + m + 1])
                done.then_inc(g_ready, 1)

            def mix(c, slot, prev, nxt, after):
                if nxt:
                    take_h2t(c + 1, 1 - slot)
                gelu(c, 0)
                if prev:
                    take_combine(c, slot)
                gelu(c, 1)
                if nxt:
                    take_logits(c + 1)
                    gelu_shared(c + 1, 1 - slot)
                if not prev:
                    take_combine(c, slot)
                if after:
                    normalise2(c + 2)

            nc.scalar.dma_start(wk_sb[:, :, :], wk).then_inc(wk_in, 16)
            nc.scalar.dma_start(vec_sb[:, :], vecs).then_inc(vec_in, 16)
            nc.scalar.dma_start(wv_sb[:, :, :], wv).then_inc(wv_in, 16)
            normalise(0)
            act.wait_ge(vec_in, 16)
            take_k(0)
            take_ht(0)
            normalise(1)
            act.wait_ge(bq_head_ready, 1)
            act.wait_ge(q_psum0[0], 1)
            for g in range(P // HD):
                done = nc.scalar.activation(qbd[:, 0, 0, g % 2, g // 2, :], b_q0[0][:, 0:CH], ACT.Identity,
                                            bias=bq_head[:, 0, g:g + 1], scale=head_of[:, g:g + 1])
            done.then_inc(q0_ready, 1)
            act.wait_ge(vbd_zeros, 1)
            take_v(0)
            with nc.scalar.Fori(0, NCH - 2) as i:
                attend(i, True, True)
            attend(NCH - 2, True, False)
            attend(NCH - 1, False, False)
            act.wait_ge(hs_ones, 1)
            gelu_shared(0, 0)
            mix(0, 0, False, True, True)
            with nc.scalar.Fori(1, NCH - 3, 2) as j:
                mix(j, 1, True, True, True)
                mix(j + 1, 0, True, True, True)
            mix(NCH - 3, 1, True, True, True)
            mix(NCH - 2, 0, True, True, False)
            mix(NCH - 1, 1, True, False, False)

        @block.vector
        def _(dve):
            V = nc.vector

            def stats_x(c, n, before):
                for t in range(TPC):
                    done = V.bn_stats(st1[:, t, :], tile(x_sb, c, t))
                done.then_inc(stats1_raw, 1)
                wait_alone(dve, stats1_raw, n, stats1_raw)
                if before is not None:
                    dve.wait_ge(p_nm1, before)
                for t in range(TPC):
                    done = V.bn_aggr(mv1[:, t, :], st1[:, t, :])
                done.then_inc(stats1, 1)

            def cap(c, b):
                dve.wait_ge(e_ready, BPC * c + b + 1)
                V.tensor_scalar(p_sb[:, b, :, :, :].rearrange("p h j s -> p (h j s)"), e_sb[:, b % 2, :],
                                e_cap[:, bass.ds(c * BPC + b, 1)], E_LO, ALU.min,
                                ALU.max).then_inc(p_ready, 1)

            def divide(c):
                dve.wait_ge(den_psum, c + 1)
                V.reciprocal(rden[:, :], b_den[:, :]).then_inc(rden_ready, 1)
                dve.wait_ge(rden_ready, c + 1)
                V.tensor_tensor(ctxn[:, :, :].rearrange("p k t -> p (k t)"), b_pv[:, :], rden[:, :],
                                ALU.mult).then_inc(ctxn_ready, 1)

            def take_delta(c):
                dve.wait_ge(o_psum, c + 1)
                V.tensor_tensor(chunk(y_sb, c).rearrange("p (t d) -> p t d", d=H),
                                b_o[:, :].rearrange("p (t d) -> p t d", d=H),
                                wobv_sb[:, :].unsqueeze(1).broadcast_to([P, TPC, H]),
                                ALU.add).then_inc(t_ready, 1)

            def delta_stats(c):
                wait_alone(dve, t_ready, c + 1, stats1_raw)
                for t in range(TPC):
                    done = V.bn_stats(sto[:, t, :], tile(y_sb, c, t))
                done.then_inc(statso_raw, 1)
                wait_alone(dve, statso_raw, c + 1, stats1_raw)
                dve.wait_ge(mvo_free, c + 1)
                for t in range(TPC):
                    done = V.bn_aggr(mvo[:, t, :], sto[:, t, :])
                done.then_inc(statso, 1)

            def add_delta(c):
                dve.wait_ge(coef_o, c + 1)
                for t in range(TPC):
                    n = bass.ds(c * TPC + t, 1)
                    done = V.scalar_tensor_tensor(u_sb[:, t, :], tile(y_sb, c, t), mean_o[:, n],
                                                  gamma_sb[:, :], ALU.subtract, ALU.mult)
                done.then_inc(u_ready, 1)
                dve.wait_ge(u_ready, c + 1)
                for t in range(TPC):
                    n = bass.ds(c * TPC + t, 1)
                    done = V.scalar_tensor_tensor(tile(y_sb, c, t), u_sb[:, t, :], coef_d[:, n],
                                                  tile(x_sb, c, t), ALU.mult, ALU.add)
                done.then_inc(y_ready, 1)

            def y_stats(c):
                wait_alone(dve, y_ready, held(dve, c + 1), stats1_raw)
                for t in range(TPC):
                    done = V.bn_stats(st2[:, t, :], tile(y_sb, c, t))
                done.then_inc(stats2_raw, 1)
                wait_alone(dve, stats2_raw, c + 1, stats1_raw)
                if not (isinstance(c, int) and c == 0):
                    dve.wait_ge(p_nm2, c)
                for t in range(TPC):
                    done = V.bn_aggr(mv2[:, t, :], st2[:, t, :])
                done.then_inc(stats2, 1)

            def attend(c, prev, after, last=False):
                if after:
                    n, before = held(dve, c + 3), held(dve, c + 2)
                cap(c, 0)
                cap(c, 1)
                if after:
                    stats_x(c + 2, n, before)
                if isinstance(c, int) and c >= NCH - 3:
                    add_delta(c - (NCH - 3))
                    y_stats(c - (NCH - 3))
                if prev:
                    take_delta(c - 1)
                    delta_stats(c - 1)
                cap(c, 2)
                cap(c, 3)
                if last:
                    choose(0)
                divide(c)

            def choose(c):
                dve.wait_ge(lt_psum, c + 1)
                V.tensor_copy(lt_sb[:, :, :].rearrange("p t e -> p (t e)"),
                              b_gt[:, CH:CH + TPC * NE]).then_inc(lt_ready, 1)
                wait_alone(dve, lt_ready, c + 1, stats1_raw)
                for t in range(TPC):
                    done = V.max(m8[:, t, :], lt_sb[:, t, :])
                done.then_inc(m8_ready, 1)
                dve.wait_ge(m8_ready, c + 1)
                V.tensor_tensor(dl[:, :].unsqueeze(2), m8[:, :, 1:2], m8[:, :, 0:1],
                                ALU.subtract).then_inc(dl_ready, 1)
                for t in range(TPC):
                    done = V.max_index(i8[:, t, :], m8[:, t, :], lt_sb[:, t, :])
                done.then_inc(i8_ready, 1)
                dve.wait_ge(i8_ready, c + 1)
                for n, eq in enumerate((eq0, eq1)):
                    done = V.tensor_tensor(eq[:, :, :], iota.unsqueeze(1).broadcast_to([P, TPC, NE]),
                                           i8[:, :, n:n + 1].broadcast_to([P, TPC, NE]), ALU.is_equal)
                done.then_inc(eq_ready, 1)

            def combine(c):
                dve.wait_ge(e2_ready, c + 1)
                V.tensor_scalar(s12[:, :], e2[:, :], 1.0, None, ALU.add).then_inc(s12_ready, 1)
                dve.wait_ge(s12_ready, c + 1)
                V.reciprocal(r1[:, :], s12[:, :]).then_inc(r1_ready, 1)
                dve.wait_ge(r1_ready, c + 1)
                V.tensor_tensor(r2[:, :], e2[:, :], r1[:, :], ALU.mult).then_inc(r2_ready, 1)
                dve.wait_ge(r2_ready, c + 1)
                dve.wait_ge(eq_ready, c + 1)
                V.tensor_tensor(w0[:, :, :], eq0[:, :, :], r1[:, :].unsqueeze(2).broadcast_to([P, TPC, NE]),
                                ALU.mult)
                V.tensor_tensor(w1[:, :, :], eq1[:, :, :], r2[:, :].unsqueeze(2).broadcast_to([P, TPC, NE]),
                                ALU.mult).then_inc(w_ready, 1)
                dve.wait_ge(w_ready, c + 1)
                V.tensor_tensor(comb[:, :, :], w0[:, :, :], w1[:, :, :], ALU.add)
                V.tensor_tensor(parts[:, :, 0, :], w0[:, :, :], w1[:, :, :], ALU.add).then_inc(rest_ready, 1)
                dve.wait_ge(rest_ready, 3 * c + 1)
                V.tensor_tensor(rest[:, :, :], comb[:, :, :], parts[:, :, 0, :],
                                ALU.subtract).then_inc(rest_ready, 1)
                dve.wait_ge(rest_ready, 3 * c + 2)
                V.tensor_copy(parts[:, :, 1, :], rest[:, :, :]).then_inc(rest_ready, 1)
                dve.wait_ge(rest_ready, 3 * c + 3)
                V.tensor_tensor(parts[:, :, 2, :], rest[:, :, :], parts[:, :, 1, :],
                                ALU.subtract).then_inc(comb_ready, 1)

            def write(c):
                dve.wait_ge(u_psum, c + 1)
                V.tensor_tensor(chunk(y_sb, c), b_u[:, :], chunk(y_sb, c), ALU.add).then_inc(out_ready, 1)

            def weigh_experts(c, half):
                dve.wait_ge(bc_psum, 2 * c + half + 1)
                dve.wait_ge(g_ready, 2 * c + half + 1)
                V.tensor_tensor(gc_sb[:, 2 * half:2 * half + 2, :].rearrange("p m t -> p (m t)"),
                                g_sb[:, 2 * half:2 * half + 2, :].rearrange("p m t -> p (m t)"),
                                b_bc[half][:, :], ALU.mult).then_inc(gc_ready, 1)

            def mix(c, nxt, after):
                combine(c)
                write(c - 1)
                if after:
                    add_delta(c + 3)
                weigh_experts(c, 0)
                weigh_experts(c, 1)
                if after:
                    y_stats(c + 3)
                if nxt:
                    choose(c + 1)

            dve.wait_ge(x0_in, 16)
            stats_x(0, 1, None)
            dve.wait_ge(ident_in, 16)
            dve.wait_ge(vec_in, 16)
            for hf in range(KT):
                done = V.tensor_scalar(bq_head[:, hf, :], head_of, vec_sb[:, C_BQ + hf:C_BQ + hf + 1], None,
                                       ALU.mult)
            done.then_inc(bq_head_ready, 1)
            dve.wait_ge(stats1, 1)
            dve.wait_ge(x1_in, 16)
            stats_x(1, 2, 1)
            V.memset(ones_bd[:, :], 0.0).then_inc(ones_set, 1)
            dve.wait_ge(ones_set, 1)
            for par in range(2):
                done = V.memset(ones_bd[S * par:S * par + S, HD * par:HD * par + HD], 1.0 + SUM_EPS)
            done.then_inc(ones_set, 1)
            V.memset(hs_sb[BOT:P, :, :], 1.0).then_inc(hs_ones, 1)
            dve.wait_ge(bq_head_ready, 1)
            dve.wait_ge(q_psum0[1], 1)
            for g in range(P // HD):
                done = V.tensor_scalar(qbd[:, 0, 1, g % 2, g // 2, :], b_q0[1][:, 0:CH],
                                       head_of[:, g:g + 1], bq_head[:, 1, g:g + 1], ALU.mult, ALU.add)
            done.then_inc(q0_ready, 1)
            dve.wait_ge(mask_in, 16 * 3)
            V.tensor_copy(mask_f[:, :], mask_i[:, :]).then_inc(cap_set, 1)
            V.tensor_scalar(rs[:, :], rs_in[:, :], 0.0, RES_MAX, ALU.max, ALU.min).then_inc(rs_set, 1)
            dve.wait_ge(cap_set, 1)
            V.tensor_scalar(mask_f[:, :], mask_f[:, :], 0.5, E_HI, ALU.is_gt, ALU.mult).then_inc(cap_set, 1)
            dve.wait_ge(rs_set, 1)
            V.tensor_tensor(rs2[:, :], rs[:, :], rs[:, :], ALU.mult).then_inc(rs_set, 1)
            dve.wait_ge(cap_set, 2)
            V.tensor_scalar(e_cap[:, :], mask_f[:, :], E_LO, None, ALU.max).then_inc(cap_set, 1)
            dve.wait_ge(cap_set, 3)
            dve.wait_ge(attn_w_in, 16 * 4)
            dve.wait_ge(bias_psum, 1)
            V.tensor_tensor(wobv_sb[:, :], b_o[:, 0:H], bo_sb[:, :], ALU.add).then_inc(bias_ready, 1)
            dve.wait_ge(x23_in, 16)
            attend(0, False, True)
            dve.wait_ge(xr_in, 16)
            dve.wait_ge(bias_ready, 1)
            dve.wait_ge(ffn_w_in, 16 * 5)
            V.tensor_copy(sel_sb[:, :, :].rearrange("p m r -> p (m r)"),
                          sel_f[:, :, :].rearrange("p m r -> p (m r)"))
            V.tensor_copy(ident_h[:, :], ident).then_inc(sel_ready, 1)
            with nc.vector.Fori(1, NCH - 3) as i:
                attend(i, True, True)
            attend(NCH - 3, True, True)
            attend(NCH - 2, True, False)
            attend(NCH - 1, True, False, True)
            combine(0)
            take_delta(NCH - 1)
            weigh_experts(0, 0)
            weigh_experts(0, 1)
            delta_stats(NCH - 1)
            add_delta(3)
            choose(1)
            y_stats(3)
            with nc.vector.Fori(1, NCH - 4, 2) as j:
                mix(j, True, True)
                mix(j + 1, True, True)
            mix(NCH - 3, True, False)
            mix(NCH - 2, True, False)
            mix(NCH - 1, False, False)
            write(NCH - 1)

        @block.gpsimd
        def _(pool):
            G = nc.gpsimd

            def coef_x(c, n, first=False):
                wait_alone(pool, stats1, n, pool_const)
                G.tensor_scalar(ve1[:, :].unsqueeze(2), mv1[:, :, 1:2], LN_EPS, 1.0, ALU.add,
                                ALU.mult).then_inc(p_ve1, 1)
                wait_alone(pool, p_ve1, n, pool_const)
                G.tensor_scalar(nm1[:, :].unsqueeze(2), mv1[:, :, 0:1], -1.0, 0.0, ALU.mult,
                                ALU.add).then_inc(p_nm1, 1)
                pool.wait_ge(p_nm1, c + 1)
                if not first:
                    pool.wait_ge(h_ready, c)
                G.tensor_tensor(rstd1[:, :], ve1[:, :], neg_half[:, :], ALU.pow).then_inc(p_pw1, 1)
                pool.wait_ge(p_pw1, c + 1)
                G.tensor_tensor(nmr1[:, :], nm1[:, :], rstd1[:, :], ALU.mult).then_inc(coef1, 1)

            def coef_delta(c):
                pool.wait_ge(h_ready, c + 1)
                G.tensor_tensor(chunk(x_sb, c).rearrange("p (t d) -> p t d", d=H),
                                chunk(x_sb, c).rearrange("p (t d) -> p t d", d=H),
                                beta_sb[:, :].unsqueeze(1).broadcast_to([P, TPC, H]),
                                ALU.add).then_inc(xb_ready, 1)
                wait_alone(pool, xb_ready, c + 1, pool_const)
                pool.wait_ge(statso, c + 1)
                G.tensor_scalar(veo[:, :].unsqueeze(2), mvo[:, :, 1:2], rs2[:, 0:1], LN_EPS, ALU.mult,
                                ALU.add).then_inc(p_veo, 1)
                pool.wait_ge(p_veo, c + 1)
                G.tensor_copy(mean_o[:, bass.ds(c * TPC, TPC)].unsqueeze(2), mvo[:, :, 0:1]).then_inc(mvo_free, 1)
                pool.wait_ge(mvo_free, c + 2)
                G.tensor_tensor(pwo[:, :], veo[:, :], neg_half[:, :], ALU.pow).then_inc(p_pwo, 1)
                pool.wait_ge(p_pwo, c + 1)
                G.tensor_tensor(coef_d[:, bass.ds(c * TPC, TPC)], pwo[:, :],
                                rs[:, 0:1].broadcast_to([P, TPC]), ALU.mult).then_inc(coef_o, 1)
                pool.wait_ge(coef_o, c + 1)

            def coef_y(c, n):
                G.tensor_scalar(ve2[:, :].unsqueeze(2), mv2[:, :, 1:2], LN_EPS, 1.0, ALU.add,
                                ALU.mult).then_inc(p_ve2, 1)
                wait_alone(pool, p_ve2, n, pool_const)
                G.tensor_scalar(nm2[:, :].unsqueeze(2), mv2[:, :, 0:1], -1.0, 0.0, ALU.mult,
                                ALU.add).then_inc(p_nm2, 1)
                pool.wait_ge(p_nm2, c + 1)
                G.tensor_tensor(rstd2[:, bass.ds(c * TPC, TPC)], ve2[:, :], neg_half[:, :],
                                ALU.pow).then_inc(p_pw2, 1)
                pool.wait_ge(p_pw2, c + 1)
                G.tensor_tensor(nmr2[:, bass.ds(c * TPC, TPC)], nm2[:, :], rstd2[:, bass.ds(c * TPC, TPC)],
                                ALU.mult).then_inc(coef2, 1)
                pool.wait_ge(coef2, c + 1)

            def attend(c, prev, after):
                if after:
                    coef_x(c + 2, held(pool, c + 3))
                    pool.wait_ge(coef1, c + 3)
                if prev:
                    coef_delta(c - 1)

            def exp_difference(c):
                pool.wait_ge(dl_ready, c + 1)
                G.tensor_tensor(e2[:, :], base_e[:, :], dl[:, :], ALU.pow).then_inc(e2_ready, 1)

            for n, (dst, value) in enumerate(((neg_half, -0.5), (base_e, float(np.e)))):
                G.memset(dst[:, :], value).then_inc(pool_const, 1)
                pool.wait_ge(pool_const, n + 1)
            G.memset(mean_o[:, :], 0.0).then_inc(mvo_free, 1)
            pool.wait_ge(mvo_free, 1)
            G.memset(vbd[:, :, :, :, :], 0.0).then_inc(vbd_zeros, 1)
            pool.wait_ge(vbd_zeros, 1)
            coef_x(0, 1, True)
            pool.wait_ge(coef1, 1)
            coef_x(1, 2)
            pool.wait_ge(coef1, 2)
            G.memset(qbd[:, 1, :, :, :, :], 0.0).then_inc(zeros_set, 1)
            pool.wait_ge(zeros_set, 1)
            attend(0, False, True)
            pool.wait_ge(xr_in, 16)
            pool.wait_ge(attn_w_in, 16 * 4)
            pool.wait_ge(rs_set, 2)
            with nc.gpsimd.Fori(1, NCH - 3) as i:
                attend(i, True, True)
            for c in range(3):
                if c == 0:
                    coef_x(NCH - 1, NCH)
                    pool.wait_ge(coef1, NCH)
                pool.wait_ge(stats2, c + 1)
                coef_y(c, c + 1)
                attend(NCH - 3 + c, True, False)
            exp_difference(0)
            pool.wait_ge(e2_ready, 1)
            coef_delta(NCH - 1)
            exp_difference(1)
            pool.wait_ge(e2_ready, 2)
            pool.wait_ge(stats2, 4)
            coef_y(3, 4)
            with nc.gpsimd.Fori(1, NCH - 3) as j:
                n = held(pool, j + 4)
                wait_alone(pool, stats2, n, pool_const)
                coef_y(j + 3, n)
                exp_difference(j + 1)
                before = held(pool, j + 2)
                wait_alone(pool, e2_ready, before, pool_const)
            for c in range(NCH - 2, NCH):
                exp_difference(c)
                pool.wait_ge(e2_ready, c + 1)


_ORDER = ["x", "ctx_t", "mask_t", "wq", "wk", "wv", "wo", "bo", "gamma", "beta", "rscale", "vecs",
          "wdn", "wsg", "wup", "w5", "ident_d", "sel_d"]


def _layout(i):
    def rows(w, n):
        return w.T.reshape(-1, P, n).transpose(1, 0, 2)

    a = {k: np.asarray(v) for k, v in i.items()}
    d = {}
    d["x"] = a["x"].reshape(TOK, H)
    d["ctx_t"] = a["ctx_2048"].reshape(NCH, CH, KT, P).transpose(0, 3, 2, 1)
    d["mask_t"] = a["mask_BxS2_ik0"].T
    for n in "qko":
        d["w" + n] = rows(a["L0_xattn_W" + n], H)
    wv = rows(a["L0_xattn_Wv"], H).reshape(P, KT, PAIRS, 2, HD)
    d["wv"] = wv.transpose(0, 1, 3, 2, 4).reshape(P, KT, H)
    d["bo"], d["gamma"], d["beta"] = a["L0_xattn_bo"], a["L0_xattn_ln_gamma"], a["L0_xattn_ln_beta"]
    d["rscale"] = a["L0_xattn_residual_scale"].reshape(1)
    bs = a["L0_ffn_bs_d"]
    d["vecs"] = np.concatenate([a["L0_xattn_bq"].reshape(KT, P), a["L0_xattn_bk"].reshape(KT, P),
                                a["L0_xattn_bv"].reshape(KT, P),
                                a["L0_ffn_bd"].reshape(PM, P), np.concatenate([bs, bs])[None]]).T
    d["wdn"] = rows(a["L0_ffn_wd"].reshape(NE * BOT, H), NE * BOT)
    d["wsg"] = rows(np.concatenate([a["L0_ffn_ws_d"], a["L0_ffn_gate_w"]]), SG)
    d["wup"] = a["L0_ffn_wu"].transpose(0, 2, 1).reshape(PM, P, H).transpose(1, 0, 2)
    d["w5"] = np.concatenate([a["L0_ffn_ws_u"].T] + [a["L0_ffn_bu"]] * NP + [a["L0_ffn_bs_u"].reshape(1, H)])
    d["ident_d"] = np.concatenate([np.eye(P, dtype=np.float32),
                                   np.tile(np.arange(NE, dtype=np.float32), (P, 1)),
                                   np.repeat(np.eye(P // HD, dtype=np.float32), HD, axis=0)], axis=1)
    sel = np.zeros((NE, PM, P), np.float32)
    for e in range(NE):
        sel[e, e // 2, BOT * (e % 2):BOT * (e % 2) + BOT] = 1.0
    d["sel_d"] = np.concatenate([sel] * NP)
    return {k: np.ascontiguousarray(v) for k, v in d.items()}


def kernel(**inputs):
    import concourse.bacc as bacc
    from concourse.bass_utils import run_bass_kernel_spmd

    nc = bacc.Bacc("TRN2", target_bir_lowering=False, num_devices=1)
    data = _layout(inputs)
    arrays, args = {}, []
    for name in _ORDER:
        arrays[f"in_{name}"] = data[name]
        args.append(nc.dram_tensor(f"in_{name}", data[name].shape, mybir.dt.from_np(data[name].dtype),
                                   kind="ExternalInput").ap())
    args.append(nc.dram_tensor("out_y", (TOK, H), mybir.dt.float32, kind="ExternalOutput").ap())
    xattn_moe(nc, *args)
    r = run_bass_kernel_spmd(nc, [arrays], core_ids=[0])
    return r.results[0]["out_y"].reshape(B, S, H)
```

```python
import numpy as np
import concourse.bass as bass
from concourse import mybir
from contextlib import ExitStack

B, S, H = 32, 64, 256
NH, HD = 16, 16
NE, BOT = 8, 64
TOK = B * S

P = 128
KT = H // P
CH = 256
NCH = TOK // CH
TPC = CH // P
BPC = CH // S
GR = 2 * CH
NG = TOK // GR
TPG = GR // P
PAIRS = NH // 2
PPH = PAIRS // KT
PM = NE * BOT // P
SG = BOT + NE
POOL_CHUNKS = (4, 6)
POOL_M = 2
NP = 3
ONES = BOT + NP * NE
LN_EPS = 1e-5
SUM_EPS = 1e-8
SCORE_SCALE = 1.0 / float(np.sqrt(HD))
E_HI = float(np.exp(50.0))
E_LO = float(np.exp(-50.0))
RES_MAX = 0.3

C_BQ, C_BK, C_BV, C_BD, C_BS, C_N = 0, KT, 2 * KT, 3 * KT, 3 * KT + PM, 3 * KT + PM + 1


def xattn_moe(nc, x, ctx_t, mask_t, wq, wk, wv, wo, bo, gamma, beta, rscale, vecs,
              wdn, wsg, wup, w5, ident_d, sel_d, out):
    f32, f32r, bf16 = mybir.dt.float32, mybir.dt.float32r, mybir.dt.bfloat16
    ALU = mybir.AluOpType
    ACT = mybir.ActivationFunctionType

    es = ExitStack()
    with es:
        def sb(name, shape, dt=f32):
            return es.enter_context(nc.sbuf_tensor(name, shape, dt))

        def sem(name):
            return es.enter_context(nc.semaphore(name))

        wq_sb, wk_sb, wo_sb = sb("wq_sb", [P, KT, H]), sb("wk_sb", [P, KT, H]), sb("wo_sb", [P, KT, H])
        wv_sb = sb("wv_sb", [P, KT, H])
        wk_hi, wk_lo = sb("wk_hi", [P, KT, H], f32r), sb("wk_lo", [P, KT, H], f32r)
        wq_hi, wq_lo = sb("wq_hi", [P, KT, H], f32r), sb("wq_lo", [P, KT, H], f32r)
        wo_hi, wo_lo = sb("wo_hi", [P, KT, H], f32r), sb("wo_lo", [P, KT, H], f32r)
        wv_hi, wv_lo = sb("wv_hi", [P, KT, H], f32r), sb("wv_lo", [P, KT, H], f32r)
        bo_sb, gamma_sb, beta_sb = sb("bo_sb", [P, H]), sb("gamma_sb", [P, H]), sb("beta_sb", [P, H])
        vec_sb = sb("vec_sb", [P, C_N])
        wdn_sb = sb("wdn_sb", [P, KT, NE * BOT])
        wsg_sb = sb("wsg_sb", [P, KT, SG])
        wdn_hi, wdn_lo = sb("wdn_hi", [P, KT, NE * BOT], f32r), sb("wdn_lo", [P, KT, NE * BOT], f32r)
        wsg_hi, wsg_lo = sb("wsg_hi", [P, KT, SG], f32r), sb("wsg_lo", [P, KT, SG], f32r)
        wup_sb = sb("wup_sb", [P, PM, H])
        wup_hi, wup_lo = sb("wup_hi", [P, PM, H], f32r), sb("wup_lo", [P, PM, H], f32r)
        w5_sb = sb("w5_sb", [ONES + 1, H])
        wobv_sb = sb("wobv_sb", [P, H])
        sel_f, sel_sb = sb("sel_f", [NP * NE, PM, P]), sb("sel_sb", [NP * NE, PM, P], bf16)
        ident_h = sb("ident_h", [P, P], bf16)
        ones_bd = sb("ones_bd", [P, 32])
        neg_half, base_e = sb("neg_half", [P, TPC]), sb("base_e", [P, TPG])
        const_sb = sb("const_sb", [P, P + NE + 2])
        ident, iota, parity = const_sb[:, 0:P], const_sb[:, P:P + NE], const_sb[:, P + NE:]
        bk_par = sb("bk_par", [P, KT, 2])
        mask_i = sb("mask_i", [P, B], mybir.dt.int32)
        mask_f = sb("mask_f", [P, B])
        e_cap = sb("e_cap", [P, B])
        rs_in, rs, rs2 = sb("rs_in", [P, 1]), sb("rs", [P, 1]), sb("rs2", [P, 1])

        x_sb = sb("x_sb", [P, NCH * TPC * H])
        y_sb = sb("y_sb", [P, NCH * TPC * H])
        ctx_sb = sb("ctx_sb", [P, KT, CH])
        ctx_hi, ctx_lo = sb("ctx_hi", [P, KT, CH], f32r), sb("ctx_lo", [P, KT, CH], f32r)
        st1, mv1 = sb("st1", [P, TPC, 6]), sb("mv1", [P, TPC, 2])
        ve1, rstd1 = sb("ve1", [P, TPC]), sb("rstd1", [P, TPC])
        nm1, nmr1 = sb("nm1", [P, TPC]), sb("nmr1", [P, TPC])
        h_sb = sb("h_sb", [P, TPC, H])
        ht_sb = sb("ht_sb", [P, KT, CH])
        ht_hi, ht_lo = sb("ht_hi", [P, KT, CH], f32r), sb("ht_lo", [P, KT, CH], f32r)
        kt_sb = sb("kt_sb", [P, KT, BPC, 2, S])
        qbd = sb("qbd", [P, 2, KT, PPH, CH])
        vbd = sb("vbd", [P, BPC, PAIRS, 2, HD])
        e_sb = sb("e_sb", [P, 2, PAIRS * S])
        p_sb = sb("p_sb", [P, BPC, KT, PPH, S])
        rden = sb("rden", [P, KT * CH])
        ctxn = sb("ctxn", [P, KT, CH])
        ctxn_hi, ctxn_lo = sb("ctxn_hi", [P, KT, CH], f32r), sb("ctxn_lo", [P, KT, CH], f32r)
        u_sb = sb("u_sb", [P, TPC, H])
        sto, mvo = sb("sto", [P, TPC, 6]), sb("mvo", [P, TPC, 2])
        veo, pwo = sb("veo", [P, TPC]), sb("pwo", [P, TPC])
        mean_o, coef_d = sb("mean_o", [P, NCH * TPC]), sb("coef_d", [P, NCH * TPC])
        st2, mv2 = sb("st2", [P, TPC, 6]), sb("mv2", [P, TPC, 2])
        ve2, nm2 = sb("ve2", [P, TPC]), sb("nm2", [P, TPC])
        rstd2, nmr2 = sb("rstd2", [P, NCH * TPC]), sb("nmr2", [P, NCH * TPC])

        h2_sb = sb("h2_sb", [P, TPG, H])
        h2t_hi, h2t_lo = sb("h2t_hi", [P, 2, KT, GR], f32r), sb("h2t_lo", [P, 2, KT, GR], f32r)
        g_sb = sb("g_sb", [P, PM, GR])
        gc_hi, gc_lo = sb("gc_hi", [P, PM, GR], f32r), sb("gc_lo", [P, PM, GR], f32r)
        hs_sb = sb("hs_sb", [P, 2, GR])
        lg_sb = sb("lg_sb", [SG, GR])
        lt_sb, m8 = sb("lt_sb", [P, TPG, NE]), sb("m8", [P, TPG, NE])
        i8 = sb("i8", [P, TPG, NE], mybir.dt.uint32)
        eq0, eq1 = sb("eq0", [P, TPG, NE]), sb("eq1", [P, TPG, NE])
        w0, w1 = sb("w0", [P, TPG, NE]), sb("w1", [P, TPG, NE])
        comb, rest = sb("comb", [P, TPG, NE]), sb("rest", [P, TPG, NE])
        parts = sb("parts", [P, TPG, NP, NE], bf16)
        cr_sb = sb("cr_sb", [NP * NE, GR], bf16)
        dl, e2 = sb("dl", [P, TPG]), sb("e2", [P, TPG])
        s12, r1, r2 = sb("s12", [P, TPG]), sb("r1", [P, TPG]), sb("r2", [P, TPG])

        banks = [es.enter_context(nc.psum_tensor(f"bank{n}", [P, 512], f32)) for n in range(8)]
        b_t, b_q, b_k, b_s, b_pv, b_den, b_o = (banks[0], banks[1], banks[2], banks[3:5], banks[5],
                                                banks[6], banks[7])
        b_q0 = (banks[6], banks[5])
        b_t2, b_sg, b_gt, b_d, b_bc = banks[0], banks[1], banks[2], banks[3:5], banks[5:7]
        b_bc_of = [(*b_bc, *b_d)] * (NG - 1) + [(*b_bc, b_sg, b_bc[0])]
        b_u = (banks[7], banks[0])
        b_ct = b_gt[0:NP * NE, 0:GR // 2].bitcast(bf16)
        b_lt = b_gt[:, GR // 2:GR // 2 + TPG * NE]

        x0_in, x1_in, x23_in, xr_in = sem("x0_in"), sem("x1_in"), sem("x23_in"), sem("xr_in")
        ident_in, wq_in, wk_in, wv_in, vec_in = (sem("ident_in"), sem("wq_in"), sem("wk_in"),
                                                 sem("wv_in"), sem("vec_in"))
        mask_in, attn_w_in, ffn_w_in = sem("mask_in"), sem("attn_w_in"), sem("ffn_w_in")
        bk_par_ready, q0_ready, k0_ready = sem("bk_par_ready"), sem("q0_ready"), sem("k0_ready")
        ctx_in, stored = sem("ctx_in"), sem("stored")
        ctxn_hi_ready, ctxn_lo_ready, wo_split = sem("ctxn_hi_ready"), sem("ctxn_lo_ready"), sem("wo_split")
        ffn_rest, wq_split = sem("ffn_rest"), sem("wq_split")
        ht_hi_ready, ht_lo_ready = sem("ht_hi_ready"), sem("ht_lo_ready")
        ctx_hi_ready, ctx_lo_ready, wkv_split = sem("ctx_hi_ready"), sem("ctx_lo_ready"), sem("wkv_split")
        q0_zeros = sem("q0_zeros")
        zeros_set, pool_const, ones_set, hs_ones, vbd_zeros, cap_set, rs_set = (
            sem("zeros_set"), sem("pool_const"), sem("ones_set"), sem("hs_ones"), sem("vbd_zeros"), sem("cap_set"),
            sem("rs_set"))
        stats1_raw, stats1, p_ve1, p_pw1, coef1 = (sem("stats1_raw"), sem("stats1"), sem("p_ve1"),
                                                   sem("p_pw1"), sem("coef1"))
        p_nm1, p_nm2, mvo_free = sem("p_nm1"), sem("p_nm2"), sem("mvo_free")
        bias_psum, bias_ready = sem("bias_psum"), sem("bias_ready")
        h_ready, t_psum, ht_ready = sem("h_ready"), sem("t_psum"), sem("ht_ready")
        q_psum, k_psum, v_psum = sem("q_psum"), sem("k_psum"), sem("v_psum")
        q_psum0 = (sem("q_psum0_a"), sem("q_psum0_b"))
        qt_ready, kt_ready, vbd_ready = sem("qt_ready"), sem("kt_ready"), sem("vbd_ready")
        s_psum, e_ready, p_ready = sem("s_psum"), sem("e_ready"), sem("p_ready")
        den_psum, rden_ready, ctxn_ready, o_psum = (sem("den_psum"), sem("rden_ready"),
                                                    sem("ctxn_ready"), sem("o_psum"))
        t_ready, statso_raw, statso = sem("t_ready"), sem("statso_raw"), sem("statso")
        p_veo, p_pwo, xb_ready, coef_o = sem("p_veo"), sem("p_pwo"), sem("xb_ready"), sem("coef_o")
        u_ready, y_ready, stats2_raw, stats2 = (sem("u_ready"), sem("y_ready"), sem("stats2_raw"),
                                                sem("stats2"))
        p_ve2, p_pw2, coef2 = sem("p_ve2"), sem("p_pw2"), sem("coef2")
        h2_ready, t2_psum, h2t_ready = sem("h2_ready"), sem("t2_psum"), sem("h2t_ready")
        h2t_hi_ready, cr_ready, split_ready = sem("h2t_hi_ready"), sem("cr_ready"), sem("split_ready")
        sg_psum, lg_ready, lt_psum, lt_ready = (sem("sg_psum"), sem("lg_ready"), sem("lt_psum"),
                                                sem("lt_ready"))
        m8_ready, i8_ready, dl_ready, e2_ready, eq_ready = (sem("m8_ready"), sem("i8_ready"),
                                                            sem("dl_ready"), sem("e2_ready"),
                                                            sem("eq_ready"))
        s12_ready, r1_ready, r2_ready, w_ready, comb_ready = (sem("s12_ready"), sem("r1_ready"),
                                                              sem("r2_ready"), sem("w_ready"),
                                                              sem("comb_ready"))
        ct_psum, ct_ready, hs_ready = sem("ct_psum"), sem("ct_ready"), sem("hs_ready")
        sel_ready, rest_ready = sem("sel_ready"), sem("rest_ready")
        d_psum, bc_psum, g_ready, gc_ready = sem("d_psum"), sem("bc_psum"), sem("g_ready"), sem("gc_ready")
        yp_norm, yp_gamma, yp_ready = sem("yp_norm"), sem("yp_gamma"), sem("yp_ready")
        gc_hi_ready, gc_lo_ready, gc_lo2_ready = sem("gc_hi_ready"), sem("gc_lo_ready"), sem("gc_lo2_ready")
        u_psum, out_ready = sem("u_psum"), sem("out_ready")

        def tile(buf, c, t):
            return buf[:, bass.ds((c * TPC + t) * H, H)]

        def chunk(buf, c):
            return buf[:, bass.ds(c * TPC * H, TPC * H)]

        def by_pool(c):
            return sum(n < c for n in POOL_CHUNKS)

        def held(engine, value):
            return value if isinstance(value, int) else engine.snap(engine.to_reg(value))

        def wait_alone(engine, signal, value, passed):
            engine.wait_ge(passed, 1)
            engine.wait_ge(signal, value)

        block = es.enter_context(nc.Block())

        @block.sync
        def _(sp):
            def load_ctx(c):
                src = ctx_t[0] if isinstance(c, int) and c == 0 else ctx_t[bass.ds(c, 1)]
                if not (isinstance(c, int) and c == 0):
                    src = src.rearrange("a p k t -> (a p) k t")
                nc.sync.dma_start(ctx_sb[:, :, :], src).then_inc(ctx_in, 16)

            xv = x.rearrange("(n p) d -> p n d", p=P)
            xs = x_sb[:, :].rearrange("p (n d) -> p n d", d=H)
            nc.sync.dma_start(xs[:, 0:TPC], xv[:, 0:TPC]).then_inc(x0_in, 16)
            load_ctx(0)
            nc.sync.dma_start(const_sb[:, :], ident_d).then_inc(ident_in, 16)
            nc.sync.dma_start(wq_sb[:, :, :], wq).then_inc(wq_in, 16)
            nc.sync.dma_start(xs[:, TPC:2 * TPC], xv[:, TPC:2 * TPC]).then_inc(x1_in, 16)
            for dst, src in ((wo_sb[:, :, :], wo), (bo_sb[:, :], bo.partition_broadcast(P)),
                             (gamma_sb[:, :], gamma.partition_broadcast(P)),
                             (beta_sb[:, :], beta.partition_broadcast(P))):
                nc.sync.dma_start(dst, src).then_inc(attn_w_in, 16)
            for dst, src in ((mask_i[0:S, :], mask_t), (mask_i[S:P, :], mask_t),
                             (rs_in[:, :], rscale.partition_broadcast(P))):
                nc.sync.dma_start(dst, src).then_inc(mask_in, 16)
            nc.sync.dma_start(xs[:, 2 * TPC:4 * TPC], xv[:, 2 * TPC:4 * TPC]).then_inc(x23_in, 16)
            nc.sync.dma_start(xs[:, 4 * TPC:], xv[:, 4 * TPC:]).then_inc(xr_in, 16)
            for dst, src in ((wdn_sb[:, :, :], wdn), (wsg_sb[:, :, :], wsg), (wup_sb[:, :, :], wup),
                             (w5_sb[:, :], w5), (sel_f[:, :, :], sel_d)):
                nc.sync.dma_start(dst, src).then_inc(ffn_w_in, 16)

            sp.wait_ge(v_psum, 1)
            load_ctx(1)
            with nc.sync.Fori(2, NCH) as i:
                sp.wait_ge(ctx_lo_ready, i - 1)
                load_ctx(i)

            with nc.sync.Fori(0, NCH) as j:
                sp.wait_ge(out_ready, j + 1)
                nc.sync.dma_start(out[bass.ds(j * CH, CH), :].rearrange("(t p) d -> p t d", p=P),
                                  chunk(y_sb, j).rearrange("p (t d) -> p t d", d=H)).then_inc(stored, 16)
            sp.wait_ge(stored, 16 * NCH)

        @block.tensor
        def _(pe):
            def matmul(o, w, m, first=True, last=True):
                return nc.tensor.matmul(o, w, m, start=first, stop=last)

            def transpose_h(c):
                pe.wait_ge(h_ready, c + 1)
                for k in range(KT):
                    for t in range(TPC):
                        o = k * CH + t * P
                        done = nc.tensor.transpose(b_t[:, o:o + P], h_sb[:, t, k * P:(k + 1) * P],
                                                   ident)
                done.then_inc(t_psum, 1)

            def project(dst, w, m_sb, done_sem):
                for m in range(KT):
                    for k in range(KT):
                        done = matmul(dst[:, m * CH:(m + 1) * CH], w[:, k, m * P:(m + 1) * P],
                                      m_sb[:, k, :], k == 0, k == KT - 1)
                done.then_inc(done_sem, 1)

            def project_parts(dst, w_hi, w_lo, m_hi, m_lo, done_sem):
                for m in range(KT):
                    o, cols = dst[:, m * CH:(m + 1) * CH], slice(m * P, (m + 1) * P)
                    for k in range(KT):
                        matmul(o, w_hi[:, k, cols], m_hi[:, k, :], k == 0, False)
                        matmul(o, w_hi[:, k, cols], m_lo[:, k, :], False, False)
                        done = matmul(o, w_lo[:, k, cols], m_hi[:, k, :], False, k == KT - 1)
                done.then_inc(done_sem, 1)

            def values(c, first=False):
                if not first:
                    pe.wait_ge(qt_ready, c)
                for g in range(BPC // 2):
                    o, keys_of = b_q[:, g * H:(g + 1) * H], slice(g * P, (g + 1) * P)
                    for k in range(KT):
                        if first:
                            done = matmul(o, ctx_sb[:, k, keys_of], wv_sb[:, k, :], k == 0, k == KT - 1)
                        else:
                            matmul(o, ctx_hi[:, k, keys_of], wv_hi[:, k, :], k == 0, False)
                            matmul(o, ctx_hi[:, k, keys_of], wv_lo[:, k, :], False, False)
                            done = matmul(o, ctx_lo[:, k, keys_of], wv_hi[:, k, :], False, k == KT - 1)
                done.then_inc(v_psum, 1)

            def scores(b, slot):
                for hf in range(KT):
                    done = matmul(b_s[b % 2][:, hf * 256:(hf + 1) * 256],
                                  kt_sb[:, hf, b, :, :].rearrange("p r s -> p (r s)"),
                                  qbd[:, slot, hf, :, b * S:(b + 1) * S])
                done.then_inc(s_psum, 1)

            def weigh(c, b):
                pe.wait_ge(p_ready, BPC * c + b + 1)
                for hf in range(KT):
                    for j in range(PPH):
                        matmul(b_pv[32 * j:32 * j + 32, (hf * BPC + b) * S:(hf * BPC + b + 1) * S],
                               vbd[:, b, hf * PPH + j, :, :], p_sb[:, b, hf, j, :])

            def denominators(c):
                for j in range(PPH):
                    for hf in range(KT):
                        done = matmul(b_den[32 * j:32 * j + 32, hf * CH:(hf + 1) * CH], ones_bd[:, :],
                                      p_sb[:, :, hf, j, :])
                done.then_inc(den_psum, 1)

            def project_out(c):
                pe.wait_ge(ctxn_hi_ready, c + 1)
                for t in range(TPC):
                    o, tok = b_o[:, t * H:(t + 1) * H], slice(t * P, (t + 1) * P)
                    for k in range(KT):
                        matmul(o, ctxn_hi[:, k, tok], wo_hi[:, k, :], k == 0, False)
                        matmul(o, ctxn_hi[:, k, tok], wo_lo[:, k, :], False, False)
                    if t == 0:
                        pe.wait_ge(ctxn_lo_ready, c + 1)
                    for k in range(KT):
                        done = matmul(o, ctxn_lo[:, k, tok], wo_hi[:, k, :], False, k == KT - 1)
                done.then_inc(o_psum, 1)

            def project_late_out(c):
                pe.wait_ge(ctxn_ready, c + 1)
                for t in range(TPC):
                    for k in range(KT):
                        done = matmul(b_o[:, t * H:(t + 1) * H], ctxn[:, k, t * P:(t + 1) * P],
                                      wo_sb[:, k, :], k == 0, k == KT - 1)
                done.then_inc(o_psum, 1)

            def queries(c, whole=False):
                pe.wait_ge(vbd_ready, c)
                if whole:
                    pe.wait_ge(ht_ready, c + 1)
                    project(b_q, wq_sb, ht_sb, q_psum)
                else:
                    pe.wait_ge(ht_hi_ready, c - 1)
                    pe.wait_ge(ht_lo_ready, c - 1)
                    project_parts(b_q, wq_hi, wq_lo, ht_hi, ht_lo, q_psum)

            def first_queries():
                pe.wait_ge(ht_ready, 1)
                for m in range(KT):
                    for k in range(KT):
                        done = matmul(b_q0[m][:, 0:CH], wq_sb[:, k, m * P:(m + 1) * P], ht_sb[:, k, :],
                                      k == 0, k == KT - 1)
                    done.then_inc(q_psum0[m], 1)

            def keys(c):
                pe.wait_ge(ctx_lo_ready, c)
                project_parts(b_k, wk_hi, wk_lo, ctx_hi, ctx_lo, k_psum)

            def attend(c, slot, prev, nxt, after=True):
                if prev:
                    pe.wait_ge(qt_ready, c)
                    pe.wait_ge(kt_ready, c)
                else:
                    pe.wait_ge(q0_ready, 2)
                    pe.wait_ge(k0_ready, 1)
                scores(0, slot)
                scores(1, slot)
                if nxt:
                    queries(c + 1, not prev)
                if not nxt:
                    transpose_h2(0)
                    project_late_out(c - 1)
                pe.wait_ge(vbd_ready, c + 1)
                weigh(c, 0)
                if not nxt:
                    transpose_h2(1)
                scores(2, slot)
                if prev and nxt:
                    project_out(c - 1)
                weigh(c, 1)
                scores(3, slot)
                if not prev:
                    pe.wait_ge(wkv_split, 4)
                if nxt:
                    keys(c + 1)
                weigh(c, 2)
                if not nxt:
                    shared_and_gates(0)
                weigh(c, 3)
                if not nxt:
                    logits_to_tokens(0)
                denominators(c)
                if after:
                    transpose_h(c + 2)
                if nxt:
                    values(c + 1)

            def bias_through_wo():
                for k in range(KT):
                    done = matmul(b_o[:, 0:H], vec_sb[:, C_BV + k:C_BV + k + 1].broadcast_to([P, P]),
                                  wo_sb[:, k, :], k == 0, k == KT - 1)
                done.then_inc(bias_psum, 1)

            def transpose_h2(c):
                pe.wait_ge(h2_ready, c + 1)
                if c:
                    pe.wait_ge(h2t_ready, c)
                for k in range(KT):
                    for t in range(TPC):
                        o = k * CH + t * P
                        done = nc.tensor.transpose(b_t2[:, o:o + P],
                                                   h2_sb[:, c % 2 * TPC + t, k * P:(k + 1) * P], ident)
                done.then_inc(t2_psum, 1)

            def matmul3(o, w_hi, w_lo, rows, slot):
                for k in range(KT):
                    matmul(o, w_hi[:, k, rows], h2t_hi[:, slot, k, :], k == 0, False)
                    matmul(o, w_hi[:, k, rows], h2t_lo[:, slot, k, :], False, False)
                    done = matmul(o, w_lo[:, k, rows], h2t_hi[:, slot, k, :], False, k == KT - 1)
                return done

            def shared_and_gates(g):
                pe.wait_ge(h2t_ready, 2 * g + 2)
                matmul3(b_sg[0:SG, :], wsg_hi, wsg_lo, slice(0, SG), g % 2).then_inc(sg_psum, 1)

            def logits_to_tokens(g):
                pe.wait_ge(lg_ready, g + 1)
                for t in range(TPG):
                    done = nc.tensor.transpose(b_lt[:, t * NE:(t + 1) * NE],
                                               lg_sb[BOT:SG, t * P:(t + 1) * P], ident[BOT:SG, BOT:SG])
                done.then_inc(lt_psum, 1)

            def combine_to_rows(g):
                pe.wait_ge(comb_ready, g + 1)
                for t in range(TPG):
                    done = nc.tensor.transpose(b_ct[:, t * P:(t + 1) * P],
                                               parts[:, t, :, :].rearrange("p n e -> p (n e)"),
                                               ident_h[:, :])
                done.then_inc(ct_psum, 1)

            def down(g, m):
                if m >= 2:
                    pe.wait_ge(g_ready, PM * g + m - 1)
                matmul3(b_d[m % 2][:, :], wdn_hi, wdn_lo, slice(m * P, (m + 1) * P),
                        g % 2).then_inc(d_psum, 1)

            def broadcast_combine(g, m):
                if m >= 2 and g < NG - 1:
                    pe.wait_ge(g_ready, PM * g + m + 1)
                if m == 3 and g == NG - 1:
                    pe.wait_ge(gc_ready, PM * g + 1)
                matmul(b_bc_of[g][m][:, :], sel_sb[:, m, :], cr_sb[:, :]).then_inc(bc_psum, 1)

            def up(g, tiles, wait=False):
                outs = [b_u[half][:, t * H:(t + 1) * H] for half, t in tiles]
                toks = [slice(half * CH + t * P, half * CH + (t + 1) * P) for half, t in tiles]
                for o, tok in zip(outs, toks):
                    matmul(o, hs_sb[0:ONES + 1, g % 2, tok], w5_sb[:, :], True, False)
                for m in range(PM):
                    if wait:
                        pe.wait_ge(gc_hi_ready, PM * g + m + 1)
                    for o, tok in zip(outs, toks):
                        matmul(o, gc_hi[:, m, tok], wup_hi[:, m, :], False, False)
                        matmul(o, gc_hi[:, m, tok], wup_lo[:, m, :], False, False)
                for m in range(PM):
                    if wait and m == POOL_M:
                        pe.wait_ge(gc_lo2_ready, g + 1)
                    elif wait:
                        pe.wait_ge(gc_lo_ready, (PM - 1) * g + m + (m < POOL_M))
                    for o, tok in zip(outs, toks):
                        done = matmul(o, gc_lo[:, m, tok], wup_hi[:, m, :], False, m == PM - 1)
                return done

            def mix(g):
                nxt = g < NG - 1
                down(g, 0)
                down(g, 1)
                if g:
                    pe.wait_ge(out_ready, 2 * g)
                if nxt:
                    transpose_h2(2 * g + 2)
                if not nxt:
                    combine_to_rows(g)
                down(g, 2)
                if g and nxt:
                    combine_to_rows(g)
                if g == 0:
                    down(g, 3)
                    transpose_h2(3)
                    project_late_out(NCH - 1)
                    combine_to_rows(g)
                else:
                    if nxt:
                        transpose_h2(2 * g + 3)
                    pe.wait_ge(cr_ready, g + 1)
                    broadcast_combine(g, 0)
                    broadcast_combine(g, 1)
                    down(g, 3)
                    broadcast_combine(g, 2)
                if nxt:
                    pe.wait_ge(hs_ready, g + 1)
                    shared_and_gates(g + 1)
                if g == 0:
                    pe.wait_ge(cr_ready, g + 1)
                    broadcast_combine(g, 0)
                    broadcast_combine(g, 1)
                    broadcast_combine(g, 2)
                broadcast_combine(g, 3)
                if g == 0:
                    pe.wait_ge(t_ready, NCH)
                pe.wait_ge(hs_ready, g + 1)
                pe.wait_ge(ct_ready, g + 1)
                up(g, [(0, 0), (1, 0)], wait=True)
                if nxt:
                    logits_to_tokens(g + 1)
                up(g, [(0, 1)]).then_inc(u_psum, 1)
                up(g, [(1, 1)]).then_inc(u_psum, 1)

            pe.wait_ge(wk_in, 16)
            pe.wait_ge(ctx_in, 16)
            for m in range(KT):
                for k in range(KT):
                    done = matmul(b_k[:, m * CH:(m + 1) * CH], wk_sb[:, k, m * P:(m + 1) * P],
                                  ctx_sb[:, k, :], k == 0, k == KT - 1)
                if m == 0:
                    pe.wait_ge(ident_in, 16)
                    transpose_h(0)
            done.then_inc(k_psum, 1)
            pe.wait_ge(wq_in, 16)
            first_queries()
            pe.wait_ge(ones_set, 2)
            pe.wait_ge(vec_in, 16)
            pe.wait_ge(attn_w_in, 16 * 4)
            bias_through_wo()
            pe.wait_ge(wv_in, 16)
            values(0, True)
            transpose_h(1)
            attend(0, 0, False, True)
            pe.wait_ge(bias_ready, 1)
            pe.wait_ge(wo_split, 2)
            pe.wait_ge(wq_split, 2)
            with nc.tensor.Fori(1, NCH - 3, 2) as i:
                attend(i, 1, True, True)
                attend(i + 1, 0, True, True)
            attend(NCH - 3, 1, True, True)
            attend(NCH - 2, 0, True, True, False)
            pe.wait_ge(ffn_w_in, 16 * 5)
            pe.wait_ge(sel_ready, 1)
            pe.wait_ge(split_ready, 3)
            pe.wait_ge(ffn_rest, 3)
            attend(NCH - 1, 1, True, False, False)
            for g in range(NG):
                mix(g)

        @block.scalar
        def _(act):
            def normalise(c):
                act.wait_ge(coef1, c + 1)
                for t in range(TPC):
                    done = nc.scalar.activation(h_sb[:, t, :], tile(x_sb, c, t), ACT.Identity,
                                                bias=nmr1[:, t:t + 1], scale=rstd1[:, t:t + 1])
                done.then_inc(h_ready, 1)

            def take_ht(c, parts=True):
                act.wait_ge(t_psum, c + 1)
                nc.scalar.activation(ht_sb[:, :, :].rearrange("p k t -> p (k t)"), b_t[:, :],
                                     ACT.Copy).then_inc(ht_ready, 1)
                if parts:
                    nc.scalar.activation(ht_hi[:, :, :].rearrange("p k t -> p (k t)"), b_t[:, :],
                                         ACT.Copy).then_inc(ht_hi_ready, 1)

            def place_q(c, slot, hf, src):
                for j in range(PPH):
                    r = slice(32 * j, 32 * j + 32)
                    done = nc.scalar.activation(qbd[r, slot, hf, j, :], src[r, :], ACT.Identity,
                                                bias=vec_sb[r, C_BQ + hf:C_BQ + hf + 1])
                return done

            def take_q(c, slot):
                act.wait_ge(q_psum, c)
                for hf in range(KT):
                    done = place_q(c, slot, hf, b_q[:, hf * CH:(hf + 1) * CH])
                done.then_inc(qt_ready, 1)

            def take_k(c):
                act.wait_ge(k_psum, c + 1)
                for hf in range(KT):
                    for par in range(2):
                        done = nc.scalar.activation(kt_sb[:, hf, :, par, :],
                                                    b_k[:, hf * CH:(hf + 1) * CH].rearrange("p (b s) -> p b s", s=S),
                                                    ACT.Identity, bias=bk_par[:, hf, par:par + 1],
                                                    scale=parity[:, par:par + 1])
                done.then_inc(kt_ready, 1)

            def take_v(c):
                act.wait_ge(v_psum, c + 1)
                for n in range(2):
                    for par in range(2):
                        for g in range(BPC // 2):
                            src = b_q[S * n:S * n + S, g * H + par * P:g * H + par * P + P]
                            done = nc.scalar.activation(vbd[S * par:S * par + S, 2 * g + n, :, par, :],
                                                        src.rearrange("p (q d) -> p q d", d=HD), ACT.Copy)
                done.then_inc(vbd_ready, 1)

            def exp(c, b):
                act.wait_ge(s_psum, BPC * c + b + 1)
                nc.scalar.activation(e_sb[:, b % 2, :], b_s[b % 2][:, :], ACT.Exp,
                                     scale=SCORE_SCALE).then_inc(e_ready, 1)

            def round_attention(c):
                act.wait_ge(ctxn_ready, c + 1)
                nc.scalar.activation(ctxn_hi[:, :, :], ctxn[:, :, :], ACT.Copy).then_inc(ctxn_hi_ready, 1)

            def attend(c, nxt, after, next_slot=None, prev=True):
                exp(c, 0)
                exp(c, 1)
                if prev and nxt:
                    round_attention(c - 1)
                if nxt:
                    take_q(c + 1, next_slot)
                if not nxt:
                    take_h2t(0)
                    take_h2t(1)
                exp(c, 2)
                exp(c, 3)
                if after:
                    normalise(c + 2)
                elif nxt:
                    normalise2(0)
                    normalise2(1)
                if not nxt:
                    take_logits(0)
                    normalise2(2)
                if nxt:
                    take_k(c + 1)
                if after:
                    take_ht(c + 2)
                if nxt:
                    take_v(c + 1)

            def normalise2(c):
                act.wait_ge(coef2, c + 1)
                for t in range(TPC):
                    n = c * TPC + t
                    done = nc.scalar.activation(h2_sb[:, n % TPG, :], tile(y_sb, c, t), ACT.Identity,
                                                bias=nmr2[:, n:n + 1], scale=rstd2[:, n:n + 1])
                done.then_inc(h2_ready, 1)

            def take_h2t(c):
                act.wait_ge(t2_psum, c + 1)
                nc.scalar.activation(h2t_hi[:, c // 2 % 2, :, c % 2 * CH:(c % 2 + 1) * CH],
                                     b_t2[:, :].rearrange("p (k t) -> p k t", k=KT),
                                     ACT.Copy).then_inc(h2t_hi_ready, 1)

            def gelu_shared(g):
                act.wait_ge(sg_psum, g + 1)
                nc.scalar.activation(hs_sb[0:BOT, g % 2, :], b_sg[0:BOT, :], ACT.Gelu,
                                     bias=vec_sb[0:BOT, C_BS:C_BS + 1]).then_inc(hs_ready, 1)

            def take_logits(g):
                act.wait_ge(sg_psum, g + 1)
                nc.scalar.activation(lg_sb[BOT:SG, :], b_sg[BOT:SG, :], ACT.Copy).then_inc(lg_ready, 1)

            def take_combine(g):
                act.wait_ge(ct_psum, g + 1)
                nc.scalar.activation(cr_sb[:, :], b_ct, ACT.Copy).then_inc(cr_ready, 1)
                nc.scalar.activation(hs_sb[BOT:ONES, g % 2, :], b_ct, ACT.Copy).then_inc(ct_ready, 1)

            def gelu(g, m):
                act.wait_ge(d_psum, PM * g + m + 1)
                nc.scalar.activation(g_sb[:, m, :], b_d[m % 2][:, :], ACT.Gelu,
                                     bias=vec_sb[:, C_BD + m:C_BD + m + 1]).then_inc(g_ready, 1)

            def round_weighed(g, m):
                act.wait_ge(gc_ready, PM * g + m + 1)
                nc.scalar.activation(gc_hi[:, m, :], g_sb[:, m, :], ACT.Copy).then_inc(gc_hi_ready, 1)

            def mix(g):
                nxt = g < NG - 1
                gelu(g, 0)
                gelu(g, 1)
                if nxt:
                    take_h2t(2 * g + 2)
                if g == 0:
                    normalise2(3)
                    gelu(g, 2)
                    gelu(g, 3)
                    take_h2t(3)
                    take_combine(g)
                else:
                    take_combine(g)
                    if nxt:
                        take_h2t(2 * g + 3)
                    gelu(g, 2)
                    round_weighed(g, 0)
                    gelu(g, 3)
                    round_weighed(g, 1)
                for m in range(2 if g else 0, PM):
                    round_weighed(g, m)
                if nxt:
                    take_logits(g + 1)
                    gelu_shared(g + 1)
                for c in (2 * g + 4, 2 * g + 5):
                    if c < NCH:
                        normalise2(c)

            nc.scalar.dma_start(wk_sb[:, :, :], wk).then_inc(wk_in, 16)
            nc.scalar.dma_start(vec_sb[:, :], vecs).then_inc(vec_in, 16)
            nc.scalar.dma_start(wv_sb[:, :, :], wv).then_inc(wv_in, 16)
            normalise(0)
            act.wait_ge(vec_in, 16)
            take_ht(0, False)
            normalise(1)
            act.wait_ge(q0_zeros, 1)
            act.wait_ge(q_psum0[0], 1)
            place_q(0, 0, 0, b_q0[0][:, 0:CH]).then_inc(q0_ready, 1)
            act.wait_ge(vbd_zeros, 1)
            take_v(0)
            take_ht(1, False)
            act.wait_ge(bk_par_ready, 1)
            act.wait_ge(zeros_set, 1)
            attend(0, True, True, 1, prev=False)
            with nc.scalar.Fori(1, NCH - 3, 2) as i:
                attend(i, True, True, 0)
                attend(i + 1, True, True, 1)
            attend(NCH - 3, True, True, 0)
            attend(NCH - 2, True, False, 1)
            attend(NCH - 1, False, False)
            act.wait_ge(hs_ones, 1)
            gelu_shared(0)
            for g in range(NG):
                mix(g)

        @block.vector
        def _(dve):
            V = nc.vector

            def stats_x(c, n, before):
                for t in range(TPC):
                    done = V.bn_stats(st1[:, t, :], tile(x_sb, c, t))
                done.then_inc(stats1_raw, 1)
                wait_alone(dve, stats1_raw, n, stats1_raw)
                if before is not None:
                    dve.wait_ge(p_nm1, before)
                for t in range(TPC):
                    done = V.bn_aggr(mv1[:, t, :], st1[:, t, :])
                done.then_inc(stats1, 1)

            def cap(c, b):
                dve.wait_ge(e_ready, BPC * c + b + 1)
                V.tensor_scalar(p_sb[:, b, :, :, :].rearrange("p h j s -> p (h j s)"), e_sb[:, b % 2, :],
                                e_cap[:, bass.ds(c * BPC + b, 1)], E_LO, ALU.min,
                                ALU.max).then_inc(p_ready, 1)

            def divide(c):
                dve.wait_ge(den_psum, c + 1)
                V.reciprocal(rden[:, :], b_den[:, :]).then_inc(rden_ready, 1)
                dve.wait_ge(rden_ready, c + 1)
                V.tensor_tensor(ctxn[:, :, :].rearrange("p k t -> p (k t)"), b_pv[:, :], rden[:, :],
                                ALU.mult).then_inc(ctxn_ready, 1)

            def take_delta(c):
                dve.wait_ge(o_psum, c + 1)
                V.tensor_tensor(chunk(y_sb, c).rearrange("p (t d) -> p t d", d=H),
                                b_o[:, :].rearrange("p (t d) -> p t d", d=H),
                                wobv_sb[:, :].unsqueeze(1).broadcast_to([P, TPC, H]),
                                ALU.add).then_inc(t_ready, 1)

            def delta_stats(c):
                wait_alone(dve, t_ready, c + 1, stats1_raw)
                for t in range(TPC):
                    done = V.bn_stats(sto[:, t, :], tile(y_sb, c, t))
                done.then_inc(statso_raw, 1)
                wait_alone(dve, statso_raw, c + 1, stats1_raw)
                dve.wait_ge(mvo_free, c + 1)
                for t in range(TPC):
                    done = V.bn_aggr(mvo[:, t, :], sto[:, t, :])
                done.then_inc(statso, 1)

            def add_delta(c):
                dve.wait_ge(coef_o, c + 1)
                for t in range(TPC):
                    n = bass.ds(c * TPC + t, 1)
                    done = V.scalar_tensor_tensor(u_sb[:, t, :], tile(y_sb, c, t), mean_o[:, n],
                                                  gamma_sb[:, :], ALU.subtract, ALU.mult)
                done.then_inc(u_ready, 1)
                dve.wait_ge(u_ready, c + 1 - by_pool(c))
                for t in range(TPC):
                    n = bass.ds(c * TPC + t, 1)
                    done = V.scalar_tensor_tensor(tile(y_sb, c, t), u_sb[:, t, :], coef_d[:, n],
                                                  tile(x_sb, c, t), ALU.mult, ALU.add)
                done.then_inc(y_ready, 1)

            def y_stats(c):
                if c in POOL_CHUNKS:
                    wait_alone(dve, yp_ready, by_pool(c) + 1, stats1_raw)
                else:
                    wait_alone(dve, y_ready, c + 1 - by_pool(c), stats1_raw)
                for t in range(TPC):
                    done = V.bn_stats(st2[:, t, :], tile(y_sb, c, t))
                done.then_inc(stats2_raw, 1)
                wait_alone(dve, stats2_raw, c + 1, stats1_raw)
                if not (isinstance(c, int) and c == 0):
                    dve.wait_ge(p_nm2, c)
                for t in range(TPC):
                    done = V.bn_aggr(mv2[:, t, :], st2[:, t, :])
                done.then_inc(stats2, 1)

            def round_weights():
                dve.wait_ge(ffn_w_in, 16 * 5)
                for hi, w in ((wdn_hi, wdn_sb), (wsg_hi, wsg_sb), (wup_hi, wup_sb)):
                    V.tensor_copy(hi[:, :, :], w[:, :, :]).then_inc(split_ready, 1)
                V.tensor_copy(sel_sb[:, :, :].rearrange("p m r -> p (m r)"),
                              sel_f[:, :, :].rearrange("p m r -> p (m r)"))
                V.tensor_copy(ident_h[:, :], ident).then_inc(sel_ready, 1)

            def split_wo_wq():
                dve.wait_ge(wq_in, 16)
                dve.wait_ge(attn_w_in, 16 * 4)
                V.tensor_copy(wo_hi[:, :, :], wo_sb[:, :, :]).then_inc(wo_split, 1)
                V.tensor_copy(wq_hi[:, :, :], wq_sb[:, :, :]).then_inc(wq_split, 1)
                dve.wait_ge(wq_split, 1)
                V.tensor_tensor(wq_lo[:, :, :], wq_sb[:, :, :], wq_hi[:, :, :].bitcast(f32),
                                ALU.subtract).then_inc(wq_split, 1)
                dve.wait_ge(wo_split, 1)
                V.tensor_tensor(wo_lo[:, :, :], wo_sb[:, :, :], wo_hi[:, :, :].bitcast(f32),
                                ALU.subtract).then_inc(wo_split, 1)

            def round_ctx(c):
                dve.wait_ge(ctx_in, 16 * (c + 1))
                wait_alone(dve, v_psum, held(dve, c), stats1_raw)
                V.tensor_copy(ctx_hi[:, :, :], ctx_sb[:, :, :]).then_inc(ctx_hi_ready, 1)

            def attend(c, prev, after, last=False):
                if after:
                    n, before = held(dve, c + 3), held(dve, c + 2)
                cap(c, 0)
                cap(c, 1)
                if not last:
                    round_ctx(c + 1)
                if after:
                    stats_x(c + 2, n, before)
                if not prev:
                    round_weights()
                if last:
                    split_h2t(0)
                if isinstance(c, int) and c >= NCH - 4:
                    add_delta(c - (NCH - 4))
                    if not last:
                        y_stats(c - (NCH - 4))
                if last:
                    take_delta(c - 1)
                    split_h2t(1)
                cap(c, 2)
                if prev and not last:
                    take_delta(c - 1)
                cap(c, 3)
                if prev:
                    delta_stats(c - 1)
                if not prev:
                    split_wo_wq()
                if last:
                    y_stats(3)
                    choose(0)
                divide(c)

            def split_h2t(c):
                dve.wait_ge(h2t_hi_ready, c + 1)
                part = (slice(0, P), c // 2 % 2, slice(0, KT), slice(c % 2 * CH, (c % 2 + 1) * CH))
                V.tensor_tensor(h2t_lo[part], b_t2[:, :].rearrange("p (k t) -> p k t", k=KT),
                                h2t_hi[part].bitcast(f32), ALU.subtract).then_inc(h2t_ready, 1)

            def choose(g):
                dve.wait_ge(lt_psum, g + 1)
                V.tensor_copy(lt_sb[:, :, :].rearrange("p t e -> p (t e)"), b_lt).then_inc(lt_ready, 1)
                dve.wait_ge(lt_ready, g + 1)
                for t in range(TPG):
                    done = V.max(m8[:, t, :], lt_sb[:, t, :])
                done.then_inc(m8_ready, 1)
                dve.wait_ge(m8_ready, g + 1)
                V.tensor_tensor(dl[:, :].unsqueeze(2), m8[:, :, 1:2], m8[:, :, 0:1],
                                ALU.subtract).then_inc(dl_ready, 1)
                for t in range(TPG):
                    done = V.max_index(i8[:, t, :], m8[:, t, :], lt_sb[:, t, :])
                done.then_inc(i8_ready, 1)
                dve.wait_ge(i8_ready, g + 1)
                for n, eq in enumerate((eq0, eq1)):
                    done = V.tensor_tensor(eq[:, :, :], iota.unsqueeze(1).broadcast_to([P, TPG, NE]),
                                           i8[:, :, n:n + 1].broadcast_to([P, TPG, NE]), ALU.is_equal)
                done.then_inc(eq_ready, 1)

            def combine(c):
                dve.wait_ge(e2_ready, c + 1)
                V.tensor_scalar(s12[:, :], e2[:, :], 1.0, None, ALU.add).then_inc(s12_ready, 1)
                dve.wait_ge(s12_ready, c + 1)
                V.reciprocal(r1[:, :], s12[:, :]).then_inc(r1_ready, 1)
                dve.wait_ge(r1_ready, c + 1)
                V.tensor_tensor(r2[:, :], e2[:, :], r1[:, :], ALU.mult).then_inc(r2_ready, 1)
                dve.wait_ge(r2_ready, c + 1)
                dve.wait_ge(eq_ready, c + 1)
                V.tensor_tensor(w0[:, :, :], eq0[:, :, :], r1[:, :].unsqueeze(2).broadcast_to([P, TPG, NE]),
                                ALU.mult)
                V.tensor_tensor(w1[:, :, :], eq1[:, :, :], r2[:, :].unsqueeze(2).broadcast_to([P, TPG, NE]),
                                ALU.mult).then_inc(w_ready, 1)
                dve.wait_ge(w_ready, c + 1)
                V.tensor_tensor(comb[:, :, :], w0[:, :, :], w1[:, :, :], ALU.add)
                V.tensor_tensor(parts[:, :, 0, :], w0[:, :, :], w1[:, :, :], ALU.add).then_inc(rest_ready, 1)
                dve.wait_ge(rest_ready, 3 * c + 1)
                V.tensor_tensor(rest[:, :, :], comb[:, :, :], parts[:, :, 0, :],
                                ALU.subtract).then_inc(rest_ready, 1)
                dve.wait_ge(rest_ready, 3 * c + 2)
                V.tensor_copy(parts[:, :, 1, :], rest[:, :, :]).then_inc(rest_ready, 1)
                dve.wait_ge(rest_ready, 3 * c + 3)
                V.tensor_tensor(parts[:, :, 2, :], rest[:, :, :], parts[:, :, 1, :],
                                ALU.subtract).then_inc(comb_ready, 1)

            def write(c):
                dve.wait_ge(u_psum, c + 1)
                V.tensor_tensor(chunk(y_sb, c), b_u[c % 2][:, :], chunk(y_sb, c),
                                ALU.add).then_inc(out_ready, 1)

            def weigh_experts(g, m):
                dve.wait_ge(bc_psum, PM * g + m + 1)
                dve.wait_ge(g_ready, PM * g + m + 1)
                V.tensor_tensor(g_sb[:, m, :], g_sb[:, m, :], b_bc_of[g][m][:, :],
                                ALU.mult).then_inc(gc_ready, 1)

            def rest_of_weighed(g, m):
                dve.wait_ge(gc_hi_ready, PM * g + m + 1)
                V.tensor_tensor(gc_lo[:, m, :], g_sb[:, m, :], gc_hi[:, m, :].bitcast(f32),
                                ALU.subtract).then_inc(gc_lo_ready, 1)

            def mix(g):
                nxt, after = g < NG - 1, g < NG - 2
                if g == 0:
                    split_h2t(2)
                    combine(0)
                    split_h2t(3)
                    take_delta(NCH - 1)
                    y_stats(4)
                    weigh_experts(g, 0)
                else:
                    if nxt:
                        split_h2t(2 * g + 2)
                    weigh_experts(g, 0)
                    if nxt:
                        split_h2t(2 * g + 3)
                weigh_experts(g, 1)
                weigh_experts(g, 2)
                if g:
                    rest_of_weighed(g, 0)
                weigh_experts(g, 3)
                if not g:
                    rest_of_weighed(g, 0)
                rest_of_weighed(g, 1)
                rest_of_weighed(g, 3)
                if after:
                    if g:
                        y_stats(2 * g + 4)
                    add_delta(2 * g + 5)
                    y_stats(2 * g + 5)
                if nxt:
                    choose(g + 1)
                write(2 * g)
                write(2 * g + 1)
                if nxt:
                    combine(g + 1)
                if g == 0:
                    delta_stats(NCH - 1)

            V.memset(qbd[:, 0, :, :, :], 0.0).then_inc(q0_zeros, 1)
            dve.wait_ge(x0_in, 16)
            stats_x(0, 1, None)
            dve.wait_ge(ident_in, 16)
            dve.wait_ge(vec_in, 16)
            for hf in range(KT):
                done = V.tensor_scalar(bk_par[:, hf, :], parity, vec_sb[:, C_BK + hf:C_BK + hf + 1], None,
                                       ALU.mult)
            done.then_inc(bk_par_ready, 1)
            dve.wait_ge(stats1, 1)
            dve.wait_ge(x1_in, 16)
            stats_x(1, 2, 1)
            dve.wait_ge(bk_par_ready, 1)
            dve.wait_ge(k_psum, 1)
            for hf in range(KT):
                for par in range(2):
                    done = V.tensor_scalar(kt_sb[:, hf, :, par, :],
                                           b_k[:, hf * CH:(hf + 1) * CH].rearrange("p (b s) -> p b s", s=S),
                                           parity[:, par:par + 1], bk_par[:, hf, par:par + 1],
                                           ALU.mult, ALU.add)
            done.then_inc(k0_ready, 1)
            V.memset(ones_bd[:, :], 0.0).then_inc(ones_set, 1)
            dve.wait_ge(ones_set, 1)
            for par in range(2):
                done = V.memset(ones_bd[S * par:S * par + S, HD * par:HD * par + HD], 1.0 + SUM_EPS)
            done.then_inc(ones_set, 1)
            V.memset(hs_sb[BOT:P, :, :], 1.0).then_inc(hs_ones, 1)
            dve.wait_ge(q0_zeros, 1)
            dve.wait_ge(q_psum0[1], 1)
            for j in range(PPH):
                r = slice(32 * j, 32 * j + 32)
                done = V.tensor_scalar(qbd[r, 0, 1, j, :], b_q0[1][r, 0:CH], 1.0,
                                       vec_sb[r, C_BQ + 1:C_BQ + 2], ALU.mult, ALU.add)
            done.then_inc(q0_ready, 1)
            dve.wait_ge(mask_in, 16 * 3)
            V.tensor_copy(mask_f[:, :], mask_i[:, :]).then_inc(cap_set, 1)
            V.tensor_scalar(rs[:, :], rs_in[:, :], 0.0, RES_MAX, ALU.max, ALU.min).then_inc(rs_set, 1)
            dve.wait_ge(cap_set, 1)
            V.tensor_scalar(mask_f[:, :], mask_f[:, :], 0.5, E_HI, ALU.is_gt, ALU.mult).then_inc(cap_set, 1)
            dve.wait_ge(rs_set, 1)
            V.tensor_tensor(rs2[:, :], rs[:, :], rs[:, :], ALU.mult).then_inc(rs_set, 1)
            dve.wait_ge(cap_set, 2)
            V.tensor_scalar(e_cap[:, :], mask_f[:, :], E_LO, None, ALU.max).then_inc(cap_set, 1)
            dve.wait_ge(cap_set, 3)
            dve.wait_ge(attn_w_in, 16 * 4)
            dve.wait_ge(bias_psum, 1)
            V.tensor_tensor(wobv_sb[:, :], b_o[:, 0:H], bo_sb[:, :], ALU.add).then_inc(bias_ready, 1)
            dve.wait_ge(wk_in, 16)
            V.tensor_copy(wk_hi[:, :, :], wk_sb[:, :, :]).then_inc(wkv_split, 1)
            dve.wait_ge(wv_in, 16)
            V.tensor_copy(wv_hi[:, :, :], wv_sb[:, :, :]).then_inc(wkv_split, 1)
            dve.wait_ge(wkv_split, 2)
            for hi, lo, w in ((wk_hi, wk_lo, wk_sb), (wv_hi, wv_lo, wv_sb)):
                V.tensor_tensor(lo[:, :, :], w[:, :, :], hi[:, :, :].bitcast(f32),
                                ALU.subtract).then_inc(wkv_split, 1)
            dve.wait_ge(x23_in, 16)
            attend(0, False, True)
            dve.wait_ge(xr_in, 16)
            dve.wait_ge(bias_ready, 1)
            with nc.vector.Fori(1, NCH - 4) as i:
                attend(i, True, True)
            attend(NCH - 4, True, True)
            attend(NCH - 3, True, True)
            attend(NCH - 2, True, False)
            attend(NCH - 1, True, False, True)
            for g in range(NG):
                mix(g)

        @block.gpsimd
        def _(pool):
            G = nc.gpsimd

            def coef_x(c, n, first=False):
                wait_alone(pool, stats1, n, pool_const)
                G.tensor_scalar(ve1[:, :].unsqueeze(2), mv1[:, :, 1:2], LN_EPS, 1.0, ALU.add,
                                ALU.mult).then_inc(p_ve1, 1)
                wait_alone(pool, p_ve1, n, pool_const)
                G.tensor_scalar(nm1[:, :].unsqueeze(2), mv1[:, :, 0:1], -1.0, 0.0, ALU.mult,
                                ALU.add).then_inc(p_nm1, 1)
                pool.wait_ge(p_nm1, c + 1)
                if not first:
                    pool.wait_ge(h_ready, c)
                G.tensor_tensor(rstd1[:, :], ve1[:, :], neg_half[:, :], ALU.pow).then_inc(p_pw1, 1)
                pool.wait_ge(p_pw1, c + 1)
                G.tensor_tensor(nmr1[:, :], nm1[:, :], rstd1[:, :], ALU.mult).then_inc(coef1, 1)

            def coef_delta(c):
                pool.wait_ge(h_ready, c + 1)
                G.tensor_tensor(chunk(x_sb, c).rearrange("p (t d) -> p t d", d=H),
                                chunk(x_sb, c).rearrange("p (t d) -> p t d", d=H),
                                beta_sb[:, :].unsqueeze(1).broadcast_to([P, TPC, H]),
                                ALU.add).then_inc(xb_ready, 1)
                wait_alone(pool, xb_ready, c + 1, pool_const)
                pool.wait_ge(statso, c + 1)
                G.tensor_scalar(veo[:, :].unsqueeze(2), mvo[:, :, 1:2], rs2[:, 0:1], LN_EPS, ALU.mult,
                                ALU.add).then_inc(p_veo, 1)
                pool.wait_ge(p_veo, c + 1)
                G.tensor_copy(mean_o[:, bass.ds(c * TPC, TPC)].unsqueeze(2), mvo[:, :, 0:1]).then_inc(mvo_free, 1)
                pool.wait_ge(mvo_free, c + 2)
                G.tensor_tensor(pwo[:, :], veo[:, :], neg_half[:, :], ALU.pow).then_inc(p_pwo, 1)
                pool.wait_ge(p_pwo, c + 1)
                G.tensor_tensor(coef_d[:, bass.ds(c * TPC, TPC)], pwo[:, :],
                                rs[:, 0:1].broadcast_to([P, TPC]), ALU.mult).then_inc(coef_o, 1)
                pool.wait_ge(coef_o, c + 1)

            def add_delta(c):
                n = by_pool(c) + 1
                for t in range(TPC):
                    i = c * TPC + t
                    G.tensor_scalar(tile(y_sb, c, t), tile(y_sb, c, t), mean_o[:, i:i + 1], coef_d[:, i:i + 1],
                                    ALU.subtract, ALU.mult).then_inc(yp_norm, 1)
                    pool.wait_ge(yp_norm, TPC * (n - 1) + t + 1)
                y_tiles = chunk(y_sb, c).rearrange("p (t d) -> p t d", d=H)
                G.tensor_tensor(y_tiles, y_tiles, gamma_sb[:, :].unsqueeze(1).broadcast_to([P, TPC, H]),
                                ALU.mult).then_inc(yp_gamma, 1)
                pool.wait_ge(yp_gamma, n)
                G.tensor_tensor(chunk(y_sb, c), chunk(y_sb, c), chunk(x_sb, c), ALU.add).then_inc(yp_ready, 1)
                pool.wait_ge(yp_ready, n)

            def coef_y(c, n):
                G.tensor_scalar(ve2[:, :].unsqueeze(2), mv2[:, :, 1:2], LN_EPS, 1.0, ALU.add,
                                ALU.mult).then_inc(p_ve2, 1)
                wait_alone(pool, p_ve2, n, pool_const)
                G.tensor_scalar(nm2[:, :].unsqueeze(2), mv2[:, :, 0:1], -1.0, 0.0, ALU.mult,
                                ALU.add).then_inc(p_nm2, 1)
                pool.wait_ge(p_nm2, c + 1)
                G.tensor_tensor(rstd2[:, bass.ds(c * TPC, TPC)], ve2[:, :], neg_half[:, :],
                                ALU.pow).then_inc(p_pw2, 1)
                pool.wait_ge(p_pw2, c + 1)
                G.tensor_tensor(nmr2[:, bass.ds(c * TPC, TPC)], nm2[:, :], rstd2[:, bass.ds(c * TPC, TPC)],
                                ALU.mult).then_inc(coef2, 1)
                pool.wait_ge(coef2, c + 1)

            def rest_of_ctx(c):
                pool.wait_ge(ctx_hi_ready, c)
                G.tensor_tensor(ctx_lo[:, :, :], ctx_sb[:, :, :], ctx_hi[:, :, :].bitcast(f32),
                                ALU.subtract).then_inc(ctx_lo_ready, 1)
                pool.wait_ge(ctx_lo_ready, c)

            def rest_of_attention(c):
                pool.wait_ge(ctxn_hi_ready, c + 1)
                G.tensor_tensor(ctxn_lo[:, :, :], ctxn[:, :, :], ctxn_hi[:, :, :].bitcast(f32),
                                ALU.subtract).then_inc(ctxn_lo_ready, 1)
                pool.wait_ge(ctxn_lo_ready, c + 1)

            def rest_of_ht(c):
                pool.wait_ge(ht_hi_ready, c - 1)
                G.tensor_tensor(ht_lo[:, :, :], ht_sb[:, :, :], ht_hi[:, :, :].bitcast(f32),
                                ALU.subtract).then_inc(ht_lo_ready, 1)
                pool.wait_ge(ht_lo_ready, c - 1)

            def weights_rest():
                pool.wait_ge(split_ready, 3)
                for n, (hi, lo, w) in enumerate(((wdn_hi, wdn_lo, wdn_sb), (wsg_hi, wsg_lo, wsg_sb),
                                                 (wup_hi, wup_lo, wup_sb))):
                    G.tensor_tensor(lo[:, :, :], w[:, :, :], hi[:, :, :].bitcast(f32),
                                    ALU.subtract).then_inc(ffn_rest, 1)
                    pool.wait_ge(ffn_rest, n + 1)

            def attend(c, prev, after, nxt=True):
                if prev and nxt:
                    rest_of_attention(c - 1)
                if nxt:
                    rest_of_ctx(c + 1)
                if after:
                    coef_x(c + 2, held(pool, c + 3))
                    pool.wait_ge(coef1, c + 3)
                if prev:
                    coef_delta(c - 1)
                if not prev:
                    weights_rest()
                if after:
                    rest_of_ht(c + 2)

            def exp_difference(c):
                pool.wait_ge(dl_ready, c + 1)
                G.tensor_tensor(e2[:, :], base_e[:, :], dl[:, :], ALU.pow).then_inc(e2_ready, 1)

            def rest_of_weighed(g):
                pool.wait_ge(gc_hi_ready, PM * g + POOL_M + 1)
                G.tensor_tensor(gc_lo[:, POOL_M, :], g_sb[:, POOL_M, :], gc_hi[:, POOL_M, :].bitcast(f32),
                                ALU.subtract).then_inc(gc_lo2_ready, 1)
                pool.wait_ge(gc_lo2_ready, g + 1)

            for n, (dst, value) in enumerate(((neg_half, -0.5), (base_e, float(np.e)))):
                G.memset(dst[:, :], value).then_inc(pool_const, 1)
                pool.wait_ge(pool_const, n + 1)
            G.memset(mean_o[:, :], 0.0).then_inc(mvo_free, 1)
            pool.wait_ge(mvo_free, 1)
            G.memset(vbd[:, :, :, :, :], 0.0).then_inc(vbd_zeros, 1)
            pool.wait_ge(vbd_zeros, 1)
            coef_x(0, 1, True)
            pool.wait_ge(coef1, 1)
            coef_x(1, 2)
            pool.wait_ge(coef1, 2)
            G.memset(qbd[:, 1, :, :, :], 0.0).then_inc(zeros_set, 1)
            pool.wait_ge(zeros_set, 1)
            attend(0, False, True)
            pool.wait_ge(xr_in, 16)
            pool.wait_ge(attn_w_in, 16 * 4)
            pool.wait_ge(rs_set, 2)
            with nc.gpsimd.Fori(1, NCH - 4) as i:
                attend(i, True, True)
            for c in range(4):
                if c < 3:
                    rest_of_attention(NCH - 5 + c)
                    rest_of_ctx(NCH - 3 + c)
                if c < 2:
                    coef_x(NCH - 2 + c, NCH - 1 + c)
                    pool.wait_ge(coef1, NCH - 1 + c)
                if c < 3:
                    pool.wait_ge(stats2, c + 1)
                    coef_y(c, c + 1)
                attend(NCH - 4 + c, True, False, False)
                if c < 2:
                    rest_of_ht(NCH - 2 + c)
            pool.wait_ge(stats2, 4)
            coef_y(3, 4)
            exp_difference(0)
            pool.wait_ge(e2_ready, 1)
            add_delta(4)
            pool.wait_ge(stats2, 5)
            coef_y(4, 5)
            rest_of_weighed(0)
            pool.wait_ge(stats2, 6)
            coef_y(5, 6)
            exp_difference(1)
            pool.wait_ge(e2_ready, 2)
            add_delta(6)
            coef_delta(NCH - 1)
            rest_of_weighed(1)
            for c in (6, 7):
                pool.wait_ge(stats2, c + 1)
                coef_y(c, c + 1)
            exp_difference(2)
            pool.wait_ge(e2_ready, 3)
            rest_of_weighed(2)
            exp_difference(3)
            pool.wait_ge(e2_ready, 4)
            rest_of_weighed(NG - 1)


_ORDER = ["x", "ctx_t", "mask_t", "wq", "wk", "wv", "wo", "bo", "gamma", "beta", "rscale", "vecs",
          "wdn", "wsg", "wup", "w5", "ident_d", "sel_d"]


def _layout(i):
    def rows(w, n):
        return w.T.reshape(-1, P, n).transpose(1, 0, 2)

    a = {k: np.asarray(v) for k, v in i.items()}
    d = {}
    d["x"] = a["x"].reshape(TOK, H)
    d["ctx_t"] = a["ctx_2048"].reshape(NCH, CH, KT, P).transpose(0, 3, 2, 1)
    d["mask_t"] = a["mask_BxS2_ik0"].T
    for n in "qko":
        d["w" + n] = rows(a["L0_xattn_W" + n], H)
    wv = rows(a["L0_xattn_Wv"], H).reshape(P, KT, PAIRS, 2, HD)
    d["wv"] = wv.transpose(0, 1, 3, 2, 4).reshape(P, KT, H)
    d["bo"], d["gamma"], d["beta"] = a["L0_xattn_bo"], a["L0_xattn_ln_gamma"], a["L0_xattn_ln_beta"]
    d["rscale"] = a["L0_xattn_residual_scale"].reshape(1)
    bs = a["L0_ffn_bs_d"]
    d["vecs"] = np.concatenate([a["L0_xattn_bq"].reshape(KT, P), a["L0_xattn_bk"].reshape(KT, P),
                                a["L0_xattn_bv"].reshape(KT, P),
                                a["L0_ffn_bd"].reshape(PM, P), np.concatenate([bs, bs])[None]]).T
    d["wdn"] = rows(a["L0_ffn_wd"].reshape(NE * BOT, H), NE * BOT)
    d["wsg"] = rows(np.concatenate([a["L0_ffn_ws_d"], a["L0_ffn_gate_w"]]), SG)
    d["wup"] = a["L0_ffn_wu"].transpose(0, 2, 1).reshape(PM, P, H).transpose(1, 0, 2)
    d["w5"] = np.concatenate([a["L0_ffn_ws_u"].T] + [a["L0_ffn_bu"]] * NP + [a["L0_ffn_bs_u"].reshape(1, H)])
    d["ident_d"] = np.concatenate([np.eye(P, dtype=np.float32),
                                   np.tile(np.arange(NE, dtype=np.float32), (P, 1)),
                                   np.tile(np.repeat(np.eye(2, dtype=np.float32), HD, axis=0), (P // HD // 2, 1))],
                                  axis=1)
    sel = np.zeros((NE, PM, P), np.float32)
    for e in range(NE):
        sel[e, e // 2, BOT * (e % 2):BOT * (e % 2) + BOT] = 1.0
    d["sel_d"] = np.concatenate([sel] * NP)
    return {k: np.ascontiguousarray(v) for k, v in d.items()}


def kernel(**inputs):
    import concourse.bacc as bacc
    from concourse.bass_utils import run_bass_kernel_spmd

    nc = bacc.Bacc("TRN2", target_bir_lowering=False, num_devices=1)
    data = _layout(inputs)
    arrays, args = {}, []
    for name in _ORDER:
        arrays[f"in_{name}"] = data[name]
        args.append(nc.dram_tensor(f"in_{name}", data[name].shape, mybir.dt.from_np(data[name].dtype),
                                   kind="ExternalInput").ap())
    args.append(nc.dram_tensor("out_y", (TOK, H), mybir.dt.float32, kind="ExternalOutput").ap())
    xattn_moe(nc, *args)
    r = run_bass_kernel_spmd(nc, [arrays], core_ids=[0])
    return r.results[0]["out_y"].reshape(B, S, H)
```
